# Optimizing a Trainium2 kernel written in Bass

```python
import numpy as np
import jax
import jax.numpy as jnp

def _softmax(x, axis=-1):
    return jax.nn.softmax(x, axis=axis)

def _gelu(x):
    return jax.nn.gelu(x, approximate=True)

def _silu(x):
    return jax.nn.silu(x)

def _sigmoid(x):
    return jax.nn.sigmoid(x)

def _layernorm(x, axis=-1, eps=1e-05):
    m = jnp.mean(x, axis=axis, keepdims=True)
    v = jnp.var(x, axis=axis, keepdims=True)
    return (x - m) / jnp.sqrt(v + eps)

def _scatter_add(tgt, idx, src, axis=0):
    return tgt.at[idx].add(src)

def _segment_sum(src, seg, n):
    return jax.ops.segment_sum(src, seg, n)
kernel_name = 'mk_adaln_ffn_d2_seqx_r4_a31564'

def setup_inputs(seed: int=0):
    np.random.seed(seed)
    _w = jnp.asarray

    def _rec_inputs():
        import jax
        import jax.numpy as jnp
        _rk = jax.random.key(seed)
        x = -7.109e-05 + 0.9999 * jax.random.normal(jax.random.fold_in(_rk, 1), (32, 64, 1024), jnp.float32)
        _lenS = 64 - jax.random.randint(jax.random.fold_in(_rk, 7), (32,), 0, max(1, 64 // 4) + 1, jnp.int32)
        _lenS2 = 64 - jax.random.randint(jax.random.fold_in(_rk, 8), (32,), 0, max(1, 64 // 4) + 1, jnp.int32)
        itok_B_0_15 = jax.random.randint(jax.random.fold_in(_rk, 11), (32,), 0, 16, jnp.int32)
        return (x, itok_B_0_15)
    x, itok_B_0_15 = _rec_inputs()

    def _L0_cond_setup():
        import jax, jax.numpy as jnp
        import numpy as np
        B, C, T = (64, 64, 1024)
        S, D = (16, 64)
        key = jax.random.key(seed)
        k1, k2, k3 = jax.random.split(key, 3)
        x = jax.random.normal(k1, (B, C, T), dtype=jnp.float32)
        condition = jax.random.randint(k2, (B,), 0, S, dtype=jnp.int64)
        bound = float(np.sqrt(6.0 / C))
        weights = jax.random.uniform(k3, (S, C, D), dtype=jnp.float32, minval=-bound, maxval=bound)
        return {'x': x, 'condition': condition, 'weights': weights}
    _L0_cond_all = _L0_cond_setup()
    _L0_cond_in = {k: v for k, v in _L0_cond_all.items() if k in ('weights',)}
    del _L0_cond_all

    def _L0_ffn_setup():
        import jax, jax.numpy as jnp
        import numpy as np
        THRESHOLD = 0.05

        def ternary_project(w, threshold=THRESHOLD, use_ste=True):
            reduce_axes = tuple(range(w.ndim - 1))
            scale = jnp.mean(jnp.abs(w), axis=reduce_axes, keepdims=True)
            ternary = jnp.where(jnp.abs(w) < threshold, 0.0, jnp.sign(w)) * scale
            if use_ste:
                return w + jax.lax.stop_gradient(ternary - w)
            return ternary
        key = jax.random.key(seed)
        kx, kw = jax.random.split(key)
        B, S, D, O = (8, 512, 1024, 1024)
        x = jax.random.normal(kx, (B, S, D), dtype=jnp.float32)
        w = jax.random.normal(kw, (D, O), dtype=jnp.float32) * 0.02
        b = jnp.zeros((O,), dtype=jnp.float32)
        return {'x': x, 'w': w, 'b': b}
    _L0_ffn_all = _L0_ffn_setup()
    _L0_ffn_in = {k: v for k, v in _L0_ffn_all.items() if k in ('w', 'b')}
    del _L0_ffn_all

    def _L1_cond_setup():
        import jax, jax.numpy as jnp
        import numpy as np
        NUM_CONDITIONS = 16
        IN_CH = 64
        OUT_CH = 64
        B = 64
        T = 1024
        key = jax.random.key(seed)
        k_x, k_w, k_c = jax.random.split(key, 3)
        x = jax.random.normal(k_x, (B, IN_CH, T), dtype=jnp.float32)
        bound = float(np.sqrt(6.0 / IN_CH))
        weights = jax.random.uniform(k_w, (NUM_CONDITIONS, IN_CH, OUT_CH), dtype=jnp.float32, minval=-bound, maxval=bound)
        condition = jax.random.randint(k_c, (B,), 0, NUM_CONDITIONS, dtype=jnp.int64)
        return {'x': x, 'weights': weights, 'condition': condition}
    _L1_cond_all = _L1_cond_setup()
    _L1_cond_in = {k: v for k, v in _L1_cond_all.items() if k in ('weights',)}
    del _L1_cond_all

    def _L1_ffn_setup():
        import jax, jax.numpy as jnp
        import numpy as np
        NF4_LEVELS = jnp.array([-1.0, -0.6961928009986877, -0.5250730514526367, -0.39491748809814453, -0.28444138169288635, -0.18477343022823334, -0.09105003625154495, 0.0, 0.07958029955625534, 0.16093020141124725, 0.24611230194568634, 0.33791524171829224, 0.44070982933044434, 0.5626170039176941, 0.7229568362236023, 1.0], dtype=jnp.float32)
        GROUP_SIZE = 64
        SCALING = 32.0 / 8.0
        key = jax.random.key(seed)
        k0, k1, k2, k3, k4, k5 = jax.random.split(key, 6)
        B, S, IN, OUT, R = (4, 512, 1024, 1024, 8)
        x = jax.random.normal(k0, (B, S, IN), dtype=jnp.float32)
        q_weight = jax.random.randint(k1, (OUT, IN), 0, 16, dtype=jnp.int32)
        q_scale = jax.random.uniform(k2, (OUT * IN // GROUP_SIZE,), dtype=jnp.float32, minval=0.005, maxval=0.05)
        bias = jax.random.normal(k3, (OUT,), dtype=jnp.float32) * 0.01
        lora_A = jax.random.normal(k4, (R, IN), dtype=jnp.float32) * 0.01
        lora_B = jax.random.normal(k5, (OUT, R), dtype=jnp.float32) * 0.01
        return {'x': x, 'q_weight': q_weight, 'q_scale': q_scale, 'bias': bias, 'lora_A': lora_A, 'lora_B': lora_B}
    _L1_ffn_all = _L1_ffn_setup()
    _L1_ffn_in = {k: v for k, v in _L1_ffn_all.items() if k in ('q_weight', 'q_scale', 'bias', 'lora_A', 'lora_B')}
    del _L1_ffn_all
    return {'x': x, 'itok_B_0_15': itok_B_0_15, 'L0_cond_weights': _L0_cond_in['weights'], 'L0_ffn_w': _L0_ffn_in['w'], 'L0_ffn_b': _L0_ffn_in['b'], 'L1_cond_weights': _L1_cond_in['weights'], 'L1_ffn_q_weight': _L1_ffn_in['q_weight'], 'L1_ffn_q_scale': _L1_ffn_in['q_scale'], 'L1_ffn_bias': _L1_ffn_in['bias'], 'L1_ffn_lora_A': _L1_ffn_in['lora_A'], 'L1_ffn_lora_B': _L1_ffn_in['lora_B']}

def reference(x, itok_B_0_15, L0_cond_weights, L0_ffn_w, L0_ffn_b, L1_cond_weights, L1_ffn_q_weight, L1_ffn_q_scale, L1_ffn_bias, L1_ffn_lora_A, L1_ffn_lora_B):
    import jax
    import jax.numpy as jnp

    def _L0_cond_ref(x, condition, weights):
        import jax, jax.numpy as jnp
        import numpy as np
        B, C, T = (64, 64, 1024)
        S, D = (16, 64)
        W = weights[condition]
        return jnp.einsum('bct,bcd->bdt', x, W)

    def _L0_ffn_ref(x, w, b):
        import jax, jax.numpy as jnp
        import numpy as np
        THRESHOLD = 0.05

        def ternary_project(w, threshold=THRESHOLD, use_ste=True):
            reduce_axes = tuple(range(w.ndim - 1))
            scale = jnp.mean(jnp.abs(w), axis=reduce_axes, keepdims=True)
            ternary = jnp.where(jnp.abs(w) < threshold, 0.0, jnp.sign(w)) * scale
            if use_ste:
                return w + jax.lax.stop_gradient(ternary - w)
            return ternary
        y = x @ ternary_project(w, threshold=THRESHOLD, use_ste=True)
        return y + b

    def _L1_cond_ref(x, weights, condition):
        import jax, jax.numpy as jnp
        import numpy as np
        NUM_CONDITIONS = 16
        IN_CH = 64
        OUT_CH = 64
        B = 64
        T = 1024
        W = weights[condition]
        return jnp.einsum('bct,bcd->bdt', x, W)

    def _L1_ffn_ref(x, q_weight, q_scale, bias, lora_A, lora_B):
        import jax, jax.numpy as jnp
        import numpy as np
        NF4_LEVELS = jnp.array([-1.0, -0.6961928009986877, -0.5250730514526367, -0.39491748809814453, -0.28444138169288635, -0.18477343022823334, -0.09105003625154495, 0.0, 0.07958029955625534, 0.16093020141124725, 0.24611230194568634, 0.33791524171829224, 0.44070982933044434, 0.5626170039176941, 0.7229568362236023, 1.0], dtype=jnp.float32)
        GROUP_SIZE = 64
        SCALING = 32.0 / 8.0
        OUT, IN = q_weight.shape
        w = NF4_LEVELS[q_weight].reshape(-1, GROUP_SIZE) * q_scale[:, None]
        w = w.reshape(OUT, IN).astype(x.dtype)
        base = jnp.einsum('bsi,oi->bso', x, w) + bias
        lora = jnp.einsum('bsr,or->bso', jnp.einsum('bsi,ri->bsr', x, lora_A), lora_B)
        return base + SCALING * lora
    x = x + _L0_ffn_ref(_L0_cond_ref(x, itok_B_0_15, L0_cond_weights), L0_ffn_w, L0_ffn_b)
    x = x + _L1_ffn_ref(_L1_cond_ref(x, L1_cond_weights, itok_B_0_15), L1_ffn_q_weight, L1_ffn_q_scale, L1_ffn_bias, L1_ffn_lora_A, L1_ffn_lora_B)
    return x

_drawn_inputs = setup_inputs


def setup_inputs(seed=0):
    import zlib

    import numpy as np

    out = dict(_drawn_inputs(seed))
    spreads = {'L0_ffn_b': (0.0, 0.1)}
    factors = {'L1_ffn_bias': 7.427}
    for name, (base, spread) in spreads.items():
        noise = np.random.default_rng([zlib.crc32(name.encode()), seed]).standard_normal(out[name].shape)
        drawn = base * np.exp(spread * noise) if base else spread * noise
        out[name] = jnp.asarray(drawn.astype(out[name].dtype))
    for name, factor in factors.items():
        out[name] = (out[name] * factor).astype(out[name].dtype)
    return out
```

```python
from contextlib import ExitStack

import numpy as np

import concourse.bass as bass
from concourse import mybir

F32 = mybir.dt.float32
F32R = mybir.dt.float32r
I32 = mybir.dt.int32
I8 = mybir.dt.int8
ALU = mybir.AluOpType
ACT = mybir.ActivationFunctionType

P = 128
BANK = 512
THRESHOLD = 0.05
LORA_SCALING = 32.0 / 8.0
NF4_LEVELS = [-1.0, -0.6961928009986877, -0.5250730514526367, -0.39491748809814453,
              -0.28444138169288635, -0.18477343022823334, -0.09105003625154495, 0.0,
              0.07958029955625534, 0.16093020141124725, 0.24611230194568634, 0.33791524171829224,
              0.44070982933044434, 0.5626170039176941, 0.7229568362236023, 1.0]
NF4_ZERO = 7


def line_through(a, level_a, b, level_b):
    f = np.float32
    want = (f(level_a), f(level_b))

    def near(v):
        up = down = f(v)
        yield up
        for _ in range(200):
            up, down = np.nextafter(up, f(9)), np.nextafter(down, f(-9))
            yield up
            yield down

    for slope in near((float(level_b) - float(level_a)) / (b - a)):
        for offset in near(float(level_a) - a * float(slope)):
            if all(f(q * float(slope) + float(offset)) == w for q, w in zip((a, b), want)):
                return float(slope), float(offset)
    raise ValueError("no such line")


def nf4_lines():
    lv = [np.float32(x) for x in NF4_LEVELS]
    z = NF4_ZERO
    above = [line_through(k, lv[z + k], k + 1, lv[z + k + 1]) for k in (1, 3, 5, 7)]
    below = [line_through(-k, -lv[z - k], -k - 1, -lv[z - k - 1]) for k in (1, 3, 5)]
    below.append((-0.5, 1.0 - 0.5 * z))
    for q in range(16):
        d = q - z
        up = max(0.0, *(np.float32(d * s + o) for s, o in above))
        down = max(0.0, *(np.float32(d * s + o) for s, o in below))
        assert np.float32(up) - np.float32(down) == lv[q]
    return above, below


def build(nc, x, itok, mix0, w0, b0, mix1, q_weight, q_scale, b1, lora_a, lora_b, out):
    B, C, T = x.shape
    NCOND = mix0.shape[0]
    G = q_scale.shape[0] * 64 // T // T * (T // 64)
    R = lora_a.shape[0]
    NT = B * C // P
    KB = T // P
    NH = T // BANK
    HB = KB // NH
    ND = KB * NH
    GH = G // NH
    NL = 4
    NC = 3
    assert C * 2 == P and NH == 2 and ND == NT and G == 16 and R == 8
    above, below = nf4_lines()

    x_v = x.rearrange("(t s) c f -> t (s c) f", s=2)
    out_v = out.rearrange("(t s) c f -> t (s c) f", s=2)
    w0_v = w0.rearrange("(k p) o -> k p o", p=P)
    q_v = q_weight.rearrange("(o p) (h i) -> o h p i", p=P, h=NH)
    scale_v = q_scale.rearrange("(o p g) -> p o g", p=P, g=G)
    lora_b_v = lora_b.rearrange("(o p) r -> p o r", p=P)

    with ExitStack() as ctx:
        def sb(name, shape, dt):
            return ctx.enter_context(nc.sbuf_tensor(name, shape, dt))

        def ps(name, shape):
            return ctx.enter_context(nc.psum_tensor(name, shape, F32))

        def sem(name):
            return ctx.enter_context(nc.semaphore(name))

        X = sb("X", [P, NT, T], F32)
        T0 = sb("T0", [P, KB, T], F32R)
        Wh = sb("Wh", [P, KB, T], F32R)
        Wl = sb("Wl", [P, KB, T], F32R)
        xh = sb("xh", [P, T], F32R)
        xl = sb("xl", [P, T], F32R)
        hh = sb("hh", [P, 2, KB, P], F32R)
        hl = sb("hl", [P, 2, KB, P], F32R)
        col_scale = sb("col_scale", [P, T], F32)
        bias = sb("bias", [P, T], F32)
        mix_raw = sb("mix_raw", [P, 2, P], F32)
        mix_h = sb("mix_h", [P, P], F32R)
        mix_l = sb("mix_l", [P, P], F32R)
        loraA = sb("loraA", [P, T], F32R)
        loraB = sb("loraB", [P, T], F32R)
        scales = sb("scales", [P, KB, G], F32)
        ident = sb("ident", [P, P], F32)
        q_raw = sb("q_raw", [P, 2, BANK], I32)
        q_mid = sb("q_mid", [P, 2, BANK], I8)
        side_p = sb("side_p", [P, 2, BANK], F32)
        side_n = sb("side_n", [P, BANK], F32)
        b_raw = sb("b_raw", [P, KB, R], F32)
        tok = sb("tok", [1, B], I32)

        def w_raw(k):
            return X[:, NT - KB + k, :]
        ones = X[:, 7, 0:P]
        a_raw = X[:, 6, :]
        b_wide = X[:, 5, :].rearrange("p (o r) -> p o r", o=KB)

        hT = [ps(f"hT{h}", [P, HB, P]) for h in range(NH)]
        hT_flat = [t[:, :, :].rearrange("p b c -> p (b c)") for t in hT]
        acc = [ps(f"acc{n}", [P, BANK]) for n in range(NH)]
        line = [ps(f"line{j}", [P, BANK]) for j in range(NC)]
        wT = ps("wT", [P, HB, P])

        s_tok = sem("s_tok")
        s_xin = [sem(f"s_xin{k}") for k in range(2)]
        s_win = [sem(f"s_win{k}") for k in range(KB)]
        s_mixin = [sem(f"s_mixin{k}") for k in range(2)]
        s_b0 = sem("s_b0")
        s_b1 = sem("s_b1")
        s_small = sem("s_small")
        s_ain = sem("s_ain")
        s_bin = sem("s_bin")
        s_qin = [sem(f"s_qin{k}") for k in range(2)]
        s_out = sem("s_out")
        s_zero = sem("s_zero")
        s_ident = sem("s_ident")
        s_settled = sem("s_settled")
        s_xh = sem("s_xh")
        s_xl = sem("s_xl")
        s_xb = sem("s_xb")
        s_mixh = sem("s_mixh")
        s_mixl = sem("s_mixl")
        s_hT = sem("s_hT")
        s_hh = sem("s_hh")
        s_hl = sem("s_hl")
        s_acc = sem("s_acc")
        s_sc = sem("s_sc")
        s_res = sem("s_res")
        s_neg = sem("s_neg")
        s_T0 = sem("s_T0")
        s_abs = sem("s_abs")
        s_sum = sem("s_sum")
        s_colsum = sem("s_colsum")
        s_colscale = sem("s_colscale")
        s_ah = sem("s_ah")
        s_al = sem("s_al")
        s_b4 = sem("s_b4")
        s_bT = sem("s_bT")
        s_loraB = sem("s_loraB")
        s_qmid = sem("s_qmid")
        s_line = sem("s_line")
        s_max = sem("s_max")
        s_lev = sem("s_lev")
        s_wn = sem("s_wn")
        s_wT = sem("s_wT")
        s_Wh = sem("s_Wh")
        s_Wl = sem("s_Wl")

        def need(eng, s, v):
            if not isinstance(v, int) or v > 0:
                eng.wait_ge(s, v)

        def tile_of(g):
            return X[:, bass.ds(g, 1), :].rearrange("p a f -> p (a f)")

        def steps(eng, one, loop):
            for layer in range(2):
                first = layer * NT
                one(first, 0, layer, True)
                one(first + 1, 1, layer, True)
                with eng.Fori(first // 2 + 1, (first + NT) // 2 - 1) as i:
                    loop["i"] = i
                    for parity in range(2):
                        one(2 * i + parity, parity, layer, False)
                one(first + NT - 2, 0, layer, True)
                one(first + NT - 1, 1, layer, True)

        LAST = 2 * NT - 1

        def exists(g):
            return not isinstance(g, int) or g <= LAST

        def layer_of(g, layer):
            return g // NT if isinstance(g, int) else layer

        block = ctx.enter_context(nc.Block())

        @block.sync
        def _(sp):
            loop = {}

            def load_x(t, parity):
                sp.dma_start(tile_of(t), x_v[bass.ds(t, 1)].rearrange("a p f -> p (a f)")
                             ).then_inc(s_xin[parity], 16)

            def load_mix(g, parity, layer):
                need(sp, s_mixl, g - 1)
                table = mix1 if layer else mix0
                t = g - layer * NT
                for s in range(2):
                    c = sp.value_load(tok[0:1, bass.ds(2 * t + s, 1)], min_val=0, max_val=NCOND - 1)
                    sp.dma_start(mix_raw[s * C:(s + 1) * C, parity, s * C:(s + 1) * C],
                                 table[bass.ds(c, 1)].rearrange("a c d -> c (a d)")
                                 ).then_inc(s_mixin[parity], 16)

            def load_q(d, o, parity):
                need(sp, s_qmid, d - 1)
                sp.dma_start(q_raw[:, parity, :], q_v[bass.ds(o, 1), parity].rearrange(
                    "a p i -> p (a i)")).then_inc(s_qin[parity], 16)

            sp.dma_start(tok[:, :], itok.rearrange("(a b) -> a b", a=1)).then_inc(s_tok, 16)
            load_x(0, 0)
            for k in range(KB):
                sp.dma_start(w_raw(k), w0_v[k]).then_inc(s_win[k], 16)
                if k == 0:
                    sp.wait_ge(s_tok, 16)
                    sp.wait_ge(s_zero, 1)
                    load_mix(0, 0, 0)
                if k == 1:
                    load_mix(1, 1, 0)
                if k == 3:
                    load_x(1, 1)
            load_q(0, 0, 0)
            load_q(1, 0, 1)

            def one(g, parity, layer, edge):
                if layer == 0:
                    if not edge or g + 2 < NT:
                        need(sp, s_xh, g + 1)
                        if edge and g < 2 or not edge:
                            need(sp, s_sum, KB if not isinstance(g, int) else min(KB, g + 1))
                        load_x(g + 2, parity)
                        o = (g + 2) // 2 if isinstance(g, int) else loop["i"] + 1
                        load_q(g + 2, o, parity)
                if exists(g + 2) if edge else True:
                    load_mix(g + 2, parity, layer_of(g + 2, layer))
                if layer == 0 and edge and g == NT - 2:
                    need(sp, s_xb, NT)
                    sp.dma_start(bias[:, :], b1.rearrange("(a f) -> a f", a=1).to_broadcast([P, T])
                                 ).then_inc(s_b1, 16)
                if layer == 1:
                    need(sp, s_res, NH * (g + 1))
                    sp.dma_start(out_v[bass.ds(g - NT, 1)].rearrange("a p f -> p (a f)"),
                                 tile_of(g - NT)).then_inc(s_out, 16)

            steps(sp, one, loop)
            sp.wait_ge(s_out, 16 * NT)

        @block.gpsimd
        def _(pool):
            def settle():
                pool.sem_inc(s_settled, 1)

            def low_x(g, layer):
                pool.wait_ge(s_xh, g + 1)
                settle()
                pool.tensor_tensor(xl[:, :], tile_of(g - layer * NT), xh[:, :].bitcast(F32),
                                   ALU.subtract).then_inc(s_xl, 1)

            def add_bias(g, layer):
                pool.wait_ge(s_xl, g + 1)
                if isinstance(g, int) and g == 0:
                    pool.wait_ge(s_b0, 16)
                if isinstance(g, int) and g == NT:
                    pool.wait_ge(s_b1, 16)
                settle()
                t = tile_of(g - layer * NT)
                pool.tensor_tensor(t, t, bias[:, :], ALU.add).then_inc(s_xb, 1)

            def middle_q(d, parity):
                pool.wait_ge(s_qin[parity], 16 * (half(d, parity) + 1))
                need(pool, s_line, 2 * NL * (d - 1))
                settle()
                pool.tensor_scalar(q_mid[:, parity, :], q_raw[:, parity, :], float(NF4_ZERO), None,
                                   ALU.subtract).then_inc(s_qmid, 1)

            loop = {}

            def half(d, parity):
                return d // 2 if isinstance(d, int) else loop["i"] + loop["ahead"]

            def weight(d, parity):
                o = d // 2 if isinstance(d, int) else loop["i"]
                lev = side_p[:, parity, :]
                pool.wait_ge(s_max, 2 * NC * (d + 1))
                settle()
                pool.tensor_tensor(lev, lev, side_n[:, :], ALU.subtract).then_inc(s_lev, 1)
                pool.wait_ge(s_lev, d + 1)
                settle()
                sc = scales[:, bass.ds(o, 1), parity * GH:(parity + 1) * GH].rearrange(
                    "p a g -> p (a g)").unsqueeze(2).to_broadcast([P, GH, BANK // GH])
                lev3 = lev.rearrange("p (g i) -> p g i", g=GH)
                pool.tensor_tensor(lev3, lev3, sc, ALU.mult).then_inc(s_wn, 1)

            pool.memset(mix_raw[:, :, :], 0.0).then_inc(s_zero, 1)
            pool.memset(X[:, 5:8, :], 0.0).then_inc(s_zero, 1)
            pool.memset(ident[:, :], 0.0).then_inc(s_zero, 1)
            pool.wait_ge(s_zero, 3)
            pool.memset(ones, 1.0).then_inc(s_zero, 1)
            pool.affine_select(out=ident[:, :], in_=ident[:, :], compare_op=ALU.not_equal, fill=1.0,
                               base=0, pattern=[[-1, P]], channel_multiplier=1).then_inc(s_ident, 1)
            low_x(0, 0)
            loop["ahead"] = 0
            middle_q(0, 0)
            for k in range(KB):
                pool.wait_ge(s_abs, max(k + 1, 2))
                if k == 1:
                    pool.tensor_tensor(col_scale[:, :], w_raw(0), w_raw(1), ALU.add).then_inc(s_sum, 2)
                if k > 1:
                    pool.wait_ge(s_sum, k)
                    pool.tensor_tensor(col_scale[:, :], col_scale[:, :], w_raw(k), ALU.add
                                       ).then_inc(s_sum, 1)
                if k == 3:
                    low_x(1, 0)
            pool.wait_ge(s_small, 16)
            add_bias(0, 0)
            add_bias(1, 0)

            def one(g, parity, layer, edge):
                ahead = g + 2
                if not edge or exists(ahead):
                    low_x(ahead, layer_of(ahead, layer))
                if layer == 0 and (not edge or g + 1 < NT):
                    loop["ahead"] = parity
                    middle_q(g + 1, 1 - parity)
                if not edge or exists(ahead):
                    add_bias(ahead, layer_of(ahead, layer))
                if layer == 0:
                    weight(g, parity)

            steps(pool, one, loop)

        @block.scalar
        def _(act):
            loop = {}

            def half(d):
                return d // 2 if isinstance(d, int) else loop["i"]

            def high_x(g, parity, layer, t_half):
                need(act, s_hT, NH * g)
                if layer == 0:
                    act.wait_ge(s_xin[parity], 16 * (t_half + 1))
                else:
                    act.wait_ge(s_res, NH * (g - NT + 1))
                act.activation(xh[:, :], tile_of(g - layer * NT), ACT.Copy).then_inc(s_xh, 1)

            def high_mix(g, parity, g_half):
                act.wait_ge(s_mixin[parity], 32 * (g_half + 1))
                need(act, s_hT, NH * g)
                act.activation(mix_h[:, :], mix_raw[:, parity, :], ACT.Copy).then_inc(s_mixh, 1)

            def high_h(g, parity):
                for h in range(NH):
                    act.wait_ge(s_hT, NH * g + h + 1)
                    if h == 0:
                        need(act, s_acc, NH * (g - 1))
                    act.activation(hh[:, parity, h * HB:(h + 1) * HB, :], hT[h][:, :, :], ACT.Copy
                                   ).then_inc(s_hh, 1)

            def lines(d, parity):
                act.wait_ge(s_qmid, d + 1)
                for side, table in enumerate((above, below)):
                    for j, (slope, offset) in enumerate(table):
                        if j == 0:
                            dst = side_n[:, :] if side else side_p[:, parity, :]
                            if side:
                                need(act, s_lev, d)
                            else:
                                need(act, s_wT, d - 1)
                        else:
                            dst = line[j - 1][:, :]
                            need(act, s_max, 2 * NC * d + NC * (side - 1) + j)
                        act.activation(dst, q_mid[:, parity, :], ACT.Copy, scale=slope, bias=offset
                                       ).then_inc(s_line, 1)

            def high_w(d, parity, o):
                act.wait_ge(s_wT, d + 1)
                act.activation(Wh[:, parity * HB:(parity + 1) * HB, bass.ds(o * P, P)], wT[:, :, :],
                               ACT.Copy).then_inc(s_Wh, 1)

            act.wait_ge(s_zero, 2)
            for r in range(4):
                act.dma_start(a_raw[32 * r:32 * r + R, :], lora_a).then_inc(s_ain, 16)
            act.dma_start(b_raw[:, :, :], lora_b_v).then_inc(s_bin, 16)
            act.dma_start(bias[:, :], b0.rearrange("(a f) -> a f", a=1).to_broadcast([P, T])
                          ).then_inc(s_b0, 16)
            act.dma_start(scales[:, :, :], scale_v).then_inc(s_small, 16)
            high_x(0, 0, 0, 0)
            high_mix(0, 0, 0)
            high_h(0, 0)
            act.wait_ge(s_ain, 64)
            act.activation(loraA[:, :], a_raw, ACT.Copy).then_inc(s_ah, 1)
            for h in range(NH):
                act.wait_ge(s_bT, h + 1)
                act.activation(loraB[:, h * BANK:(h + 1) * BANK], acc[h][:, :], ACT.Copy
                               ).then_inc(s_loraB, 1)
            for k in range(KB):
                act.wait_ge(s_T0, k + 1)
                act.activation(w_raw(k), w_raw(k), ACT.Abs).then_inc(s_abs, 1)
                if k == 3:
                    high_x(1, 1, 0, 0)
                    high_mix(1, 1, 0)
            for n in range(NH):
                act.wait_ge(s_colsum, n + 1)
                act.activation(col_scale[:, n * BANK:(n + 1) * BANK],
                               hT_flat[n],
                               ACT.Copy, scale=1.0 / T).then_inc(s_colscale, 1)

            def one(g, parity, layer, edge):
                if not edge or exists(g + 1):
                    high_h(g + 1, 1 - parity)
                if not edge or exists(g + 2):
                    gh = half(g) + 1
                    high_x(g + 2, parity, layer_of(g + 2, layer), gh)
                    high_mix(g + 2, parity, gh)
                if layer == 0:
                    lines(g, parity)
                    if not edge or g >= 1:
                        high_w(g - 1, 1 - parity, (g - 1) // 2 if edge else loop["i"] - 1 + parity)
                if layer == 1 and edge and g == NT:
                    high_w(ND - 1, 1, KB - 1)

            steps(act, one, loop)

        @block.vector
        def _(dve):
            loop = {}

            def low_mix(g, parity):
                dve.wait_ge(s_mixh, g + 1)
                dve.tensor_tensor(mix_l[:, :], mix_raw[:, parity, :], mix_h[:, :].bitcast(F32),
                                  ALU.subtract).then_inc(s_mixl, 1)

            def low_h(g, parity):
                for h in range(NH):
                    dve.wait_ge(s_hh, NH * g + h + 1)
                    blocks = slice(h * HB, (h + 1) * HB)
                    dve.tensor_tensor(hl[:, parity, blocks, :], hT[h][:, :, :],
                                      hh[:, parity, blocks, :].bitcast(F32), ALU.subtract
                                      ).then_inc(s_hl, 1)

            def result(g, n, layer):
                t = tile_of(g - layer * NT)[:, n * BANK:(n + 1) * BANK]
                dve.wait_ge(s_acc, NH * g + n + 1)
                if layer == 0:
                    if isinstance(g, int) and g == 0:
                        dve.wait_ge(s_colscale, n + 1)
                    cols = col_scale[:, n * BANK:(n + 1) * BANK]
                    dve.tensor_tensor(acc[n][:, :], acc[n][:, :], cols, ALU.mult).then_inc(s_sc, 1)
                    dve.wait_ge(s_sc, NH * g + n + 1)
                dve.wait_ge(s_xb, g + 1)
                dve.tensor_tensor(t, t, acc[n][:, :], ALU.add).then_inc(s_res, 1)

            def maxima(d, parity, side):
                dst = side_n[:, :] if side else side_p[:, parity, :]
                for j in range(NC):
                    dve.wait_ge(s_line, 2 * NL * d + NL * side + j + 2)
                    if j == 0:
                        ins = dve.scalar_tensor_tensor(dst, dst, 0.0, line[j][:, :], ALU.max, ALU.max)
                    else:
                        dve.wait_ge(s_max, 2 * NC * d + NC * side + j)
                        ins = dve.tensor_tensor(dst, dst, line[j][:, :], ALU.max)
                    ins.then_inc(s_max, 1)

            def low_w(d, parity, o):
                dve.wait_ge(s_Wh, d + 1)
                part = (slice(None), slice(parity * HB, (parity + 1) * HB), bass.ds(o * P, P))
                dve.tensor_tensor(Wl[part], wT[:, :, :], Wh[part].bitcast(F32), ALU.subtract
                                  ).then_inc(s_Wl, 1)

            dve.wait_ge(s_bin, 16)
            dve.wait_ge(s_zero, 2)
            dve.tensor_scalar(b_raw[:, :, :], b_raw[:, :, :], LORA_SCALING, None, ALU.mult
                              ).then_inc(s_b4, 1)
            dve.wait_ge(s_b4, 1)
            for c in (0, 64):
                dve.tensor_copy(b_wide[:, :, c:c + R].bitcast(F32R), b_raw[:, :, :]).then_inc(s_b4, 1)
            dve.wait_ge(s_b4, 3)
            for c in (32, 96):
                dve.tensor_tensor(b_wide[:, :, c:c + R], b_raw[:, :, :], b_wide[:, :, 0:R],
                                  ALU.subtract).then_inc(s_b4, 1)
            low_mix(0, 0)
            low_h(0, 0)
            dve.wait_ge(s_ah, 1)
            dve.tensor_tensor(loraA[64:P, :], a_raw[64:P, :], loraA[64:P, :].bitcast(F32),
                              ALU.subtract).then_inc(s_al, 1)
            for k in range(KB):
                dve.wait_ge(s_win[k], 16)
                dve.tensor_scalar(T0[:, k, :], w_raw(k), -THRESHOLD, None, ALU.is_le
                                  ).then_inc(s_neg, 1)
                dve.wait_ge(s_neg, k + 1)
                dve.scalar_tensor_tensor(T0[:, k, :], w_raw(k), THRESHOLD, T0[:, k, :].bitcast(F32),
                                         ALU.is_ge, ALU.subtract).then_inc(s_T0, 1)
                if k == 4:
                    low_mix(1, 1)

            def one(g, parity, layer, edge):
                if not edge or g >= 1:
                    before = g - 1
                    result(before, 1, layer_of(before, layer))
                if not edge or exists(g + 1):
                    low_h(g + 1, 1 - parity)
                if not edge or exists(g + 2):
                    low_mix(g + 2, parity)
                if layer == 0:
                    maxima(g, parity, 0)
                result(g, 0, layer)
                if layer == 0:
                    maxima(g, parity, 1)
                    if not edge or g >= 1:
                        low_w(g - 1, 1 - parity, (g - 1) // 2 if edge else loop["i"] - 1 + parity)
                if layer == 1 and edge and g == NT:
                    low_w(ND - 1, 1, KB - 1)

            steps(dve, one, loop)
            result(LAST, 1, 1)

        @block.tensor
        def _(pe):
            loop = {}

            def mix(g):
                pe.wait_ge(s_xl, g + 1)
                pe.wait_ge(s_mixl, g + 1)
                need(pe, s_hl, NH * g)
                for k in range(KB):
                    dst = hT[k // HB][:, k % HB, :]
                    cols = slice(k * P, (k + 1) * P)
                    pe.matmul(dst, xh[:, cols], mix_h[:, :], start=True, stop=False)
                    pe.matmul(dst, xl[:, cols], mix_h[:, :], start=False, stop=False)
                    mm = pe.matmul(dst, xh[:, cols], mix_l[:, :], start=False, stop=True)
                    if k % HB == HB - 1:
                        mm.then_inc(s_hT, 1)

            def main(g, n, parity, layer):
                cols = slice(n * BANK, (n + 1) * BANK)
                need(pe, s_res, NH * g + n - 1)
                if n == 0:
                    pe.wait_ge(s_hl, NH * (g + 1))
                if layer == 0:
                    terms = [(hh, T0), (hl, T0)]
                else:
                    terms = [(hh, Wh), (hl, Wh), (hh, Wl)]
                for k in range(KB):
                    if isinstance(g, int) and g == 0:
                        pe.wait_ge(s_T0, k + 1)
                    if isinstance(g, int) and g == NT and k % HB == 0:
                        pe.wait_ge(s_Wl, ND // NH * (n + 1) - 1 + k // HB)
                    for j, (a, b) in enumerate(terms):
                        mm = pe.matmul(acc[n][:, :], a[:, parity, k, :], b[:, k, cols],
                                       start=(k == 0 and j == 0),
                                       stop=(k == KB - 1 and j == len(terms) - 1))
                mm.then_inc(s_acc, 1)

            def turn_w(d, parity, o):
                pe.wait_ge(s_wn, d + 1)
                need(pe, s_Wl, d)
                for j in range(HB):
                    k = parity * HB + j
                    pe.matmul(wT[:, j, :], side_p[:, parity, j * P:(j + 1) * P], ident[:, :],
                              is_transpose=True, start=True, stop=False)
                    mm = pe.matmul(wT[:, j, :], loraA[:, k * P:(k + 1) * P],
                                   loraB[:, bass.ds(o * P, P)], start=False, stop=True)
                mm.then_inc(s_wT, 1)

            mix(0)
            pe.wait_ge(s_ident, 1)
            pe.wait_ge(s_b4, 5)
            for o in range(KB):
                mm = pe.transpose(acc[o // HB][:, o % HB * P:(o % HB + 1) * P], b_wide[:, o, :],
                                  ident[:, :])
                if o % HB == HB - 1:
                    mm.then_inc(s_bT, 1)
            pe.wait_ge(s_al, 1)

            def one(g, parity, layer, edge):
                if edge and g == 0:
                    pe.wait_ge(s_loraB, NH)
                    main(0, 0, 0, 0)
                    main(0, 1, 0, 0)
                    pe.wait_ge(s_sum, KB)
                    pe.wait_ge(s_zero, 4)
                    pe.wait_ge(s_hl, NH)
                    for n in range(NH):
                        pe.matmul(hT_flat[n], ones, col_scale[:, n * BANK:(n + 1) * BANK],
                                  start=True, stop=True).then_inc(s_colsum, 1)
                    pe.wait_ge(s_colscale, NH)
                    mix(1)
                    return
                if not edge or exists(g + 1):
                    mix(g + 1)
                if layer == 1 and edge and g == NT:
                    turn_w(ND - 1, 1, KB - 1)
                main(g, 0, parity, layer)
                if layer == 0:
                    turn_w(g - 1, 1 - parity, (g - 1) // 2 if edge else loop["i"] - 1 + parity)
                main(g, 1, parity, layer)

            steps(pe, one, loop)


def kernel(**inputs):
    import numpy as _np
    import concourse.bacc as _bacc
    from concourse import mybir as _mybir
    from concourse.bass_utils import run_bass_kernel_spmd as _run

    names = ["x", "itok_B_0_15", "L0_cond_weights", "L0_ffn_w", "L0_ffn_b", "L1_cond_weights",
             "L1_ffn_q_weight", "L1_ffn_q_scale", "L1_ffn_bias", "L1_ffn_lora_A", "L1_ffn_lora_B"]
    nc = _bacc.Bacc("TRN2", target_bir_lowering=False, num_devices=1, dynamic_dma_scratch_size=1024)
    arrays, args = {}, []
    for name in names:
        a = _np.ascontiguousarray(inputs[name])
        arrays[f"in_{name}"] = a
        args.append(nc.dram_tensor(f"in_{name}", a.shape, _mybir.dt.from_np(a.dtype),
                                   kind="ExternalInput").ap())
    shape = arrays["in_x"].shape
    args.append(nc.dram_tensor("out_0", shape, _mybir.dt.float32, kind="ExternalOutput").ap())
    build(nc, *args)
    r = _run(nc, [arrays], core_ids=[0])
    return r.results[0]["out_0"]
```

```python
from contextlib import ExitStack

import numpy as np

import concourse.bass as bass
from concourse import mybir

F32 = mybir.dt.float32
F32R = mybir.dt.float32r
I32 = mybir.dt.int32
I8 = mybir.dt.int8
ALU = mybir.AluOpType
ACT = mybir.ActivationFunctionType

P = 128
BANK = 512
THRESHOLD = 0.05
LORA_SCALING = 32.0 / 8.0
NF4_LEVELS = [-1.0, -0.6961928009986877, -0.5250730514526367, -0.39491748809814453,
              -0.28444138169288635, -0.18477343022823334, -0.09105003625154495, 0.0,
              0.07958029955625534, 0.16093020141124725, 0.24611230194568634, 0.33791524171829224,
              0.44070982933044434, 0.5626170039176941, 0.7229568362236023, 1.0]
NF4_ZERO = 7


def line_through(a, level_a, b, level_b):
    f = np.float32
    want = (f(level_a), f(level_b))

    def near(v):
        up = down = f(v)
        yield up
        for _ in range(200):
            up, down = np.nextafter(up, f(9)), np.nextafter(down, f(-9))
            yield up
            yield down

    for slope in near((float(level_b) - float(level_a)) / (b - a)):
        for offset in near(float(level_a) - a * float(slope)):
            if all(f(q * float(slope) + float(offset)) == w for q, w in zip((a, b), want)):
                return float(slope), float(offset)
    raise ValueError("no such line")


def nf4_lines():
    lv = [np.float32(x) for x in NF4_LEVELS]
    z = NF4_ZERO
    above = [line_through(k, lv[z + k], k + 1, lv[z + k + 1]) for k in (1, 3, 5, 7)]
    below = [line_through(-k, -lv[z - k], -k - 1, -lv[z - k - 1]) for k in (1, 3, 5)]
    below.append((-0.5, 1.0 - 0.5 * z))
    for q in range(16):
        d = q - z
        up = max(0.0, *(np.float32(d * s + o) for s, o in above))
        down = max(0.0, *(np.float32(d * s + o) for s, o in below))
        assert np.float32(up) - np.float32(down) == lv[q]
    return above, below


def build(nc, x, itok, mix0, w0, b0, mix1, q_weight, q_scale, b1, lora_a, lora_b, out):
    B, C, T = x.shape
    NCOND = mix0.shape[0]
    G = q_scale.shape[0] * 64 // T // T * (T // 64)
    R = lora_a.shape[0]
    NT = B * C // P
    KB = T // P
    NH = T // BANK
    HB = KB // NH
    ND = KB * NH
    GH = G // NH
    NL = 4
    NC = NL - 1
    LR = 2
    assert C * 2 == P and NH == 2 and ND == NT and G == 16 and R == 8
    above, below = nf4_lines()

    x_v = x.rearrange("(t s) c f -> t (s c) f", s=2)
    out_v = out.rearrange("(t s) c f -> t (s c) f", s=2)
    w0_v = w0.rearrange("(k p) o -> k p o", p=P)
    q_v = q_weight.rearrange("(o p) (h i) -> o h p i", p=P, h=NH)
    scale_v = q_scale.rearrange("(o p g) -> p o g", p=P, g=G)
    lora_b_v = lora_b.rearrange("(o p) r -> p o r", p=P)

    with ExitStack() as ctx:
        def sb(name, shape, dt):
            return ctx.enter_context(nc.sbuf_tensor(name, shape, dt))

        def ps(name, shape):
            return ctx.enter_context(nc.psum_tensor(name, shape, F32))

        def sem(name):
            return ctx.enter_context(nc.semaphore(name))

        X = sb("X", [P, NT, T], F32)
        xin = sb("xin", [P, 2, T], F32)
        T0 = sb("T0", [P, KB, T], F32R)
        Wh = sb("Wh", [P, KB, T], F32R)
        Wl = sb("Wl", [P, KB, T], F32R)
        hh = sb("hh", [P, 2, KB, P], F32R)
        hl = sb("hl", [P, 2, KB, P], F32R)
        ys = sb("ys", [P, BANK], F32)
        yh = sb("yh", [P, NH, BANK], F32R)
        yl = sb("yl", [P, NH, BANK], F32R)
        col_scale = sb("col_scale", [P, T], F32)
        bias = sb("bias", [P, T], F32)
        mix_raw = sb("mix_raw", [P, P], F32)
        mix_h = sb("mix_h", [P, 2, P], F32R)
        mix_l = sb("mix_l", [P, 2, P], F32R)
        loraA = sb("loraA", [P, T], F32R)
        loraB = sb("loraB", [P, T], F32R)
        scales = sb("scales", [P, KB, G], F32)
        ident = sb("ident", [P, P], F32)
        q_raw = sb("q_raw", [P, BANK], I32)
        q_mid = sb("q_mid", [P, 2, BANK], I8)
        side_p = sb("side_p", [P, 2, BANK], F32)
        side_n = sb("side_n", [P, BANK], F32)
        tok = sb("tok", [1, B], I32)

        def w_raw(k):
            return X[:, NT - KB + k, :]
        ones = X[:, 7, 0:P]
        a_raw = X[:, 6, :]
        b_wide = X[:, 5, :].rearrange("p (o r) -> p o r", o=KB)
        b_raw = X[:, 4, 0:KB * R].rearrange("p (o r) -> p o r", o=KB)

        xT = [ps(f"xT{h}", [P, HB, P]) for h in range(NH)]
        acc = [ps(f"acc{n}", [P, BANK]) for n in range(NH)]
        z = ps("z", [P, BANK])
        wT = ps("wT", [P, HB, P])
        line = [ps(f"line{j}", [P, BANK]) for j in range(LR)]
        wT_flat = wT[:, :, :].rearrange("p b c -> p (b c)")
        xT_flat = xT[1][:, :, :].rearrange("p b c -> p (b c)")
        col_sum = [wT_flat, xT_flat]

        s_tok = sem("s_tok")
        s_xin = [sem(f"s_xin{k}") for k in range(2)]
        s_win = [sem(f"s_win{k}") for k in range(KB)]
        s_mixin = sem("s_mixin")
        s_b0 = sem("s_b0")
        s_b1 = sem("s_b1")
        s_scales = sem("s_scales")
        s_ain = sem("s_ain")
        s_bin = sem("s_bin")
        s_qin = sem("s_qin")
        s_out = sem("s_out")
        s_zero = sem("s_zero")
        s_ident = sem("s_ident")
        s_fill = sem("s_fill")
        s_settled = sem("s_settled")
        s_xb = sem("s_xb")
        s_xT = sem("s_xT")
        s_hh = sem("s_hh")
        s_hl = sem("s_hl")
        s_acc = sem("s_acc")
        s_ys = sem("s_ys")
        s_yh = sem("s_yh")
        s_ylt0 = sem("s_ylt0")
        s_yl0 = sem("s_yl0")
        s_yl1 = sem("s_yl1")
        s_mixh = sem("s_mixh")
        s_mixl = sem("s_mixl")
        s_z = sem("s_z")
        s_zs = sem("s_zs")
        s_res = sem("s_res")
        s_neg = sem("s_neg")
        s_T0 = sem("s_T0")
        s_abs = sem("s_abs")
        s_sum = sem("s_sum")
        s_colsum = sem("s_colsum")
        s_colscale = sem("s_colscale")
        s_ah = sem("s_ah")
        s_al = sem("s_al")
        s_b4 = sem("s_b4")
        s_bT = sem("s_bT")
        s_loraB = sem("s_loraB")
        s_qmid = sem("s_qmid")
        s_line = sem("s_line")
        s_max = sem("s_max")
        s_lev = sem("s_lev")
        s_wn = sem("s_wn")
        s_wT = sem("s_wT")
        s_Wh = sem("s_Wh")
        s_Wl = sem("s_Wl")

        LAST = 2 * NT - 1

        def need(eng, s, v):
            if not isinstance(v, int) or v > 0:
                eng.wait_ge(s, v)

        def tile_of(g, layer):
            return X[:, bass.ds(g - layer * NT, 1), :].rearrange("p a f -> p (a f)")

        def half_of(g, layer, n):
            return tile_of(g, layer)[:, n * BANK:(n + 1) * BANK]

        def exists(g):
            return not isinstance(g, int) or 0 <= g <= LAST

        def layer_of(g, layer):
            return g // NT if isinstance(g, int) else layer

        def has_piece(d, layer):
            return 0 <= d < ND if isinstance(d, int) else layer == 0

        def steps(eng, one, loop):
            for layer in range(2):
                first = layer * NT
                one(first, 0, layer)
                one(first + 1, 1, layer)
                with eng.Fori(first // 2 + 1, (first + NT) // 2 - 1) as i:
                    loop["i"] = i
                    for parity in range(2):
                        one(2 * i + parity, parity, layer)
                one(first + NT - 2, 0, layer)
                one(first + NT - 1, 1, layer)

        def half_index(g, off, parity, loop):
            if isinstance(g, int):
                return (g + off) // 2
            return loop["i"] + (parity + off) // 2

        block = ctx.enter_context(nc.Block())

        @block.sync
        def _(sp):
            loop = {}

            def load_x(g, parity, layer):
                need(sp, s_xT, NH * (g - 1))
                need(sp, s_xb, g - 1)
                if layer == 0:
                    src = x_v[bass.ds(g, 1)].rearrange("a p f -> p (a f)")
                else:
                    sp.wait_ge(s_res, NH * (g - NT + 1))
                    src = tile_of(g, layer)
                sp.dma_start(xin[:, parity, :], src).then_inc(s_xin[parity], 16)

            def load_mix(g, layer):
                need(sp, s_mixl, g)
                table = mix1 if layer else mix0
                for s in range(2):
                    c = sp.value_load(tok[0:1, bass.ds(2 * (g - layer * NT) + s, 1)],
                                      min_val=0, max_val=NCOND - 1)
                    sp.dma_start(mix_raw[s * C:(s + 1) * C, s * C:(s + 1) * C],
                                 table[bass.ds(c, 1)].rearrange("a c d -> c (a d)")
                                 ).then_inc(s_mixin, 16)

            def load_q(d, o, parity):
                need(sp, s_qmid, d)
                sp.dma_start(q_raw[:, :], q_v[bass.ds(o, 1), parity].rearrange("a p i -> p (a i)")
                             ).then_inc(s_qin, 16)

            def store(g):
                sp.wait_ge(s_res, NH * (g + 1))
                sp.dma_start(out_v[bass.ds(g - NT, 1)].rearrange("a p f -> p (a f)"),
                             tile_of(g, 1)).then_inc(s_out, 16)

            load_x(0, 0, 0)
            for k in range(KB):
                sp.dma_start(w_raw(k), w0_v[k]).then_inc(s_win[k], 16)
                if k == 1:
                    sp.dma_start(tok[:, :], itok.rearrange("(a b) -> a b", a=1)).then_inc(s_tok, 16)
            load_x(1, 1, 0)
            load_q(0, 0, 0)
            sp.wait_ge(s_tok, 16)
            sp.wait_ge(s_fill, 4)
            load_mix(0, 0)
            for r in range(4):
                sp.dma_start(a_raw[32 * r:32 * r + R, :], lora_a).then_inc(s_ain, 16)
            sp.dma_start(scales[:, :, :], scale_v).then_inc(s_scales, 16)

            def one(g, parity, layer):
                if exists(g + 2):
                    load_x(g + 2, parity, layer_of(g + 2, layer))
                if isinstance(g, int) and g == 0:
                    load_q(1, 0, 1)
                if layer == 0 and isinstance(g, int) and g == NT - 2:
                    sp.wait_ge(s_xb, NT)
                    sp.dma_start(bias[:, :], b1.rearrange("(a f) -> a f", a=1).to_broadcast([P, T])
                                 ).then_inc(s_b1, 16)
                if exists(g + 1):
                    load_mix(g + 1, layer_of(g + 1, layer))
                if layer == 0 and not (isinstance(g, int) and g + 2 >= ND):
                    load_q(g + 2, half_index(g, 2, parity, loop), parity)
                if layer == 1 and not (isinstance(g, int) and g - 2 < NT):
                    store(g - 2)

            steps(sp, one, loop)
            store(LAST - 1)
            store(LAST)
            sp.wait_ge(s_out, 16 * NT)

        @block.gpsimd
        def _(pool):
            loop = {}

            def settle():
                pool.sem_inc(s_settled, 1)

            def add_bias(g, parity, layer):
                pool.wait_ge(s_xin[parity], 16 * ((g // 2 if isinstance(g, int) else loop["gi"])
                                                  + 1))
                if isinstance(g, int) and g == 0:
                    pool.wait_ge(s_b0, 16)
                if isinstance(g, int) and g == NT:
                    pool.wait_ge(s_b1, 16)
                settle()
                pool.tensor_tensor(tile_of(g, layer), xin[:, parity, :], bias[:, :], ALU.add
                                   ).then_inc(s_xb, 1)

            def low_y(g, n):
                pool.wait_ge(s_yh, NH * g + n + 1)
                settle()
                pool.tensor_tensor(yl[:, n, :], ys[:, :], yh[:, n, :].bitcast(F32), ALU.subtract
                                   ).then_inc(s_yl0, 1)

            def weight(d, parity, o):
                lev = side_p[:, parity, :]
                pool.wait_ge(s_max, 2 * NC * (d + 1))
                settle()
                pool.tensor_tensor(lev, lev, side_n[:, :], ALU.subtract).then_inc(s_lev, 1)
                pool.wait_ge(s_lev, d + 1)
                settle()
                sc = scales[:, bass.ds(o, 1), parity * GH:(parity + 1) * GH].rearrange(
                    "p a g -> p (a g)").unsqueeze(2).to_broadcast([P, GH, BANK // GH])
                lev3 = lev.rearrange("p (g i) -> p g i", g=GH)
                pool.tensor_tensor(lev3, lev3, sc, ALU.mult).then_inc(s_wn, 1)

            pool.memset(ident[:, :], 0.0).then_inc(s_zero, 1)
            pool.wait_ge(s_zero, 1)
            pool.affine_select(out=ident[:, :], in_=ident[:, :], compare_op=ALU.not_equal, fill=1.0,
                               base=0, pattern=[[-1, P]], channel_multiplier=1).then_inc(s_ident, 1)
            add_bias(0, 0, 0)
            for k in range(1, KB):
                pool.wait_ge(s_abs, k + 1)
                if k == 1:
                    pool.tensor_tensor(col_scale[:, :], w_raw(0), w_raw(1), ALU.add
                                       ).then_inc(s_sum, 2)
                else:
                    pool.wait_ge(s_sum, k)
                    pool.tensor_tensor(col_scale[:, :], col_scale[:, :], w_raw(k), ALU.add
                                       ).then_inc(s_sum, 1)
            pool.wait_ge(s_scales, 16)

            def one(g, parity, layer):
                if exists(g + 1):
                    loop["gi"] = half_index(g, 1, parity, loop)
                    add_bias(g + 1, 1 - parity, layer_of(g + 1, layer))
                if layer == 0:
                    tile_0 = isinstance(g, int) and g == 0
                    if not tile_0:
                        low_y(g, 0)
                    weight(g, parity, half_index(g, 0, parity, loop))
                    if not tile_0:
                        low_y(g, 1)

            steps(pool, one, loop)

        @block.scalar
        def _(act):
            loop = {}

            def high_x(g, parity):
                for h in range(NH):
                    act.wait_ge(s_xT, NH * g + h + 1)
                    if h == 0:
                        need(act, s_acc, NH * (g - 1))
                    act.activation(hh[:, parity, h * HB:(h + 1) * HB, :], xT[h][:, :, :], ACT.Copy
                                   ).then_inc(s_hh, 1)

            def high_mix(g, parity):
                act.wait_ge(s_mixin, 32 * (g + 1))
                need(act, s_z, NH * (g - 1))
                act.activation(mix_h[:, parity, :], mix_raw[:, :], ACT.Copy).then_inc(s_mixh, 1)

            def high_y(g, n, layer):
                m = NH * g + n
                need(act, s_z, m - 1)
                if layer == 0 and not (isinstance(g, int) and g == 0):
                    act.wait_ge(s_ys, m - NH + 1)
                    src = ys[:, :]
                else:
                    act.wait_ge(s_acc, m + 1)
                    src = acc[n][:, :]
                act.activation(yh[:, n, :], src, ACT.Copy).then_inc(s_yh, 1)

            def lines(d, parity, start, stop):
                if start == 0:
                    act.wait_ge(s_qin, 16 * (d + 1))
                    need(act, s_line, 2 * NL * (d - 1))
                    act.activation(q_mid[:, parity, :], q_raw[:, :], ACT.Copy,
                                   bias=-float(NF4_ZERO)).then_inc(s_qmid, 1)
                    act.wait_ge(s_qmid, d + 1)
                for number in range(start, stop):
                    side, j = divmod(number, NL)
                    slope, offset = (above, below)[side][j]
                    if j == 0 and side == 0:
                        need(act, s_wT, d - 1)
                        dst = side_p[:, parity, :]
                    elif j == 0:
                        need(act, s_lev, d)
                        dst = side_n[:, :]
                    else:
                        c = NC * side + j - 1
                        need(act, s_max, 2 * NC * d + c - LR + 1)
                        if isinstance(d, int) and d == 0:
                            act.wait_ge(s_loraB, NH)
                        dst = line[c % LR][:, :]
                    act.activation(dst, q_mid[:, parity, :], ACT.Copy, scale=slope, bias=offset
                                   ).then_inc(s_line, 1)

            def high_w(d, parity, o):
                act.wait_ge(s_wT, d + 1)
                act.activation(Wh[:, parity * HB:(parity + 1) * HB, bass.ds(o * P, P)], wT[:, :, :],
                               ACT.Copy).then_inc(s_Wh, 1)

            act.dma_start(b_raw, lora_b_v).then_inc(s_bin, 16)
            act.dma_start(bias[:, :], b0.rearrange("(a f) -> a f", a=1).to_broadcast([P, T])
                          ).then_inc(s_b0, 16)
            high_x(0, 0)
            for h in range(NH):
                act.wait_ge(s_bT, h + 1)
                act.activation(loraB[:, h * BANK:(h + 1) * BANK], line[h][:, :], ACT.Copy
                               ).then_inc(s_loraB, 1)
            for k in range(KB):
                act.wait_ge(s_T0, k + 1)
                if k == KB - 1:
                    high_x(1, 1)
                act.activation(w_raw(k), w_raw(k), ACT.Abs).then_inc(s_abs, 1)

            def one(g, parity, layer):
                first = isinstance(g, int) and g == 0
                if first:
                    for n in range(NH):
                        high_y(0, n, 0)
                    high_x(2, 0)
                    act.wait_ge(s_ain, 64)
                    act.activation(loraA[:, :], a_raw, ACT.Copy).then_inc(s_ah, 1)
                elif exists(g + 1) and not (isinstance(g, int) and g == 1):
                    high_x(g + 1, 1 - parity)
                high_mix(g, parity)
                if layer == 0:
                    lines(g, parity, 0, 4)
                if isinstance(g, int) and g == 1:
                    for n in range(NH):
                        act.wait_ge(s_colsum, n + 1)
                        act.activation(col_scale[:, n * BANK:(n + 1) * BANK], col_sum[n], ACT.Copy,
                                       scale=1.0 / T).then_inc(s_colscale, 1)
                if not first:
                    high_y(g, 0, layer)
                if layer == 0:
                    lines(g, parity, 4, 6)
                if has_piece(g - 1, layer):
                    high_w(g - 1, 1 - parity, half_index(g, -1, parity, loop))
                if layer == 0:
                    lines(g, parity, 6, 8)
                if not first:
                    high_y(g, 1, layer)

            steps(act, one, loop)

        @block.vector
        def _(dve):
            loop = {}

            def low_mix(g, parity):
                dve.wait_ge(s_mixh, g + 1)
                dve.tensor_tensor(mix_l[:, parity, :], mix_raw[:, :],
                                  mix_h[:, parity, :].bitcast(F32), ALU.subtract
                                  ).then_inc(s_mixl, 1)

            def low_x(g, parity):
                for h in range(NH):
                    dve.wait_ge(s_hh, NH * g + h + 1)
                    blocks = slice(h * HB, (h + 1) * HB)
                    dve.tensor_tensor(hl[:, parity, blocks, :], xT[h][:, :, :],
                                      hh[:, parity, blocks, :].bitcast(F32), ALU.subtract
                                      ).then_inc(s_hl, 1)

            def leave_y(g, n, layer):
                m = NH * g + n
                if isinstance(g, int) and g == 0:
                    dve.wait_ge(s_yh, n + 1)
                    dve.tensor_tensor(yl[:, n, :], acc[n][:, :], yh[:, n, :].bitcast(F32),
                                      ALU.subtract).then_inc(s_ylt0, 1)
                elif layer == 0:
                    dve.wait_ge(s_acc, m + 1)
                    need(dve, s_yl0, m - NH)
                    if isinstance(g, int) and g == 1:
                        dve.wait_ge(s_colscale, n + 1)
                    dve.tensor_tensor(ys[:, :], acc[n][:, :],
                                      col_scale[:, n * BANK:(n + 1) * BANK], ALU.mult
                                      ).then_inc(s_ys, 1)
                else:
                    dve.wait_ge(s_yh, m + 1)
                    dve.tensor_tensor(yl[:, n, :], acc[n][:, :], yh[:, n, :].bitcast(F32),
                                      ALU.subtract).then_inc(s_yl1, 1)

            def result(g, n, layer):
                dve.wait_ge(s_z, NH * g + n + 1)
                dve.wait_ge(s_xb, g + 1)
                t = half_of(g, layer, n)
                dve.tensor_tensor(t, t, z[:, :], ALU.add).then_inc(s_res, 1)

            def scale_z(n):
                dve.wait_ge(s_z, n + 1)
                dve.wait_ge(s_colscale, n + 1)
                dve.tensor_tensor(z[:, :], z[:, :], col_scale[:, n * BANK:(n + 1) * BANK],
                                  ALU.mult).then_inc(s_zs, 1)
                dve.wait_ge(s_zs, n + 1)

            def maxima(d, parity, start, stop):
                for c in range(start, stop):
                    side, j = divmod(c, NC)
                    dst = side_n[:, :] if side else side_p[:, parity, :]
                    dve.wait_ge(s_line, 2 * NL * d + NL * side + j + 2)
                    if j == 0:
                        ins = dve.scalar_tensor_tensor(dst, dst, 0.0, line[c % LR][:, :],
                                                       ALU.max, ALU.max)
                    else:
                        dve.wait_ge(s_max, 2 * NC * d + c)
                        ins = dve.tensor_tensor(dst, dst, line[c % LR][:, :], ALU.max)
                    ins.then_inc(s_max, 1)

            def low_w(d, parity, o):
                dve.wait_ge(s_Wh, d + 1)
                part = (slice(None), slice(parity * HB, (parity + 1) * HB), bass.ds(o * P, P))
                dve.tensor_tensor(Wl[part], wT[:, :, :], Wh[part].bitcast(F32), ALU.subtract
                                  ).then_inc(s_Wl, 1)

            for where, value in ((X[:, 5, :], 0.0), (mix_raw[:, :], 0.0), (ones, 1.0),
                                 (a_raw, 0.0)):
                dve.memset(where, value).then_inc(s_fill, 1)
            dve.wait_ge(s_bin, 16)
            dve.wait_ge(s_fill, 1)
            dve.tensor_scalar(b_raw, b_raw, LORA_SCALING, None, ALU.mult).then_inc(s_b4, 1)
            dve.wait_ge(s_b4, 1)
            for c in (0, 64):
                dve.tensor_copy(b_wide[:, :, c:c + R].bitcast(F32R), b_raw).then_inc(s_b4, 1)
            dve.wait_ge(s_b4, 3)
            for c in (32, 96):
                dve.tensor_tensor(b_wide[:, :, c:c + R], b_raw, b_wide[:, :, 0:R],
                                  ALU.subtract).then_inc(s_b4, 1)
            for k in range(KB):
                dve.wait_ge(s_win[k], 16)
                dve.tensor_scalar(T0[:, k, :], w_raw(k), -THRESHOLD, None, ALU.is_le
                                  ).then_inc(s_neg, 1)
                dve.wait_ge(s_neg, k + 1)
                dve.scalar_tensor_tensor(T0[:, k, :], w_raw(k), THRESHOLD, T0[:, k, :].bitcast(F32),
                                         ALU.is_ge, ALU.subtract).then_inc(s_T0, 1)
                if k == 0:
                    low_x(0, 0)
            low_x(1, 1)

            def one(g, parity, layer):
                first = isinstance(g, int) and g == 0
                if first:
                    for n in range(NH):
                        leave_y(0, n, 0)
                    low_x(2, 0)
                if exists(g - 2):
                    result(g - 2, 1, layer_of(g - 2, layer))
                if exists(g + 1) and not (isinstance(g, int) and g < 2):
                    low_x(g + 1, 1 - parity)
                low_mix(g, parity)
                if layer == 0:
                    maxima(g, parity, 0, 1)
                if not first:
                    leave_y(g, 0, layer)
                if layer == 0:
                    maxima(g, parity, 1, 2)
                if isinstance(g, int) and g == 1:
                    scale_z(0)
                if exists(g - 1):
                    result(g - 1, 0, layer_of(g - 1, layer))
                if layer == 0:
                    maxima(g, parity, 2, 4)
                if has_piece(g - 1, layer):
                    low_w(g - 1, 1 - parity, half_index(g, -1, parity, loop))
                if layer == 0:
                    maxima(g, parity, 4, 6)
                if first:
                    dve.wait_ge(s_ah, 1)
                    dve.tensor_tensor(loraA[64:P, :], a_raw[64:P, :], loraA[64:P, :].bitcast(F32),
                                      ALU.subtract).then_inc(s_al, 1)
                else:
                    leave_y(g, 1, layer)
                if isinstance(g, int) and g == 1:
                    scale_z(1)

            steps(dve, one, loop)
            result(LAST - 1, 1, 1)
            result(LAST, 0, 1)
            result(LAST, 1, 1)

        @block.tensor
        def _(pe):
            loop = {}

            def turn_x(g, parity):
                pe.wait_ge(s_xin[parity], 16 * ((g // 2 if isinstance(g, int) else loop["gi"]) + 1))
                need(pe, s_hl, NH * g)
                for k in range(KB):
                    mm = pe.transpose(xT[k // HB][:, k % HB, :], xin[:, parity, k * P:(k + 1) * P],
                                      ident[:, :])
                    if k % HB == HB - 1:
                        mm.then_inc(s_xT, 1)

            def main(g, n, parity, layer):
                cols = slice(n * BANK, (n + 1) * BANK)
                before = layer_of(g - 1, layer)
                if isinstance(g, int) and g == 1:
                    pe.wait_ge(s_ylt0, n + 1)
                elif before == 0:
                    pe.wait_ge(s_ys, NH * (g - 2) + n + 1)
                else:
                    pe.wait_ge(s_yl1, NH * (g - 1 - NT) + n + 1)
                if n == 0:
                    pe.wait_ge(s_hl, NH * (g + 1))
                if layer == 0:
                    terms = [(hh, T0), (hl, T0)]
                else:
                    terms = [(hh, Wh), (hl, Wh), (hh, Wl)]
                for k in range(KB):
                    if isinstance(g, int) and g == NT and k % HB == 0:
                        pe.wait_ge(s_Wl, ND // NH * (n + 1) - 1 + k // HB)
                    for j, (a, b) in enumerate(terms):
                        mm = pe.matmul(acc[n][:, :], a[:, parity, k, :], b[:, k, cols],
                                       start=(k == 0 and j == 0),
                                       stop=(k == KB - 1 and j == len(terms) - 1))
                mm.then_inc(s_acc, 1)

            def main_first():
                pe.wait_ge(s_hl, NH)
                for k in range(KB):
                    if k == KB - 2:
                        turn_x(1, 1)
                    pe.wait_ge(s_T0, k + 1)
                    for n in range(NH):
                        for a in (hh, hl):
                            mm = pe.matmul(acc[n][:, :], a[:, 0, k, :],
                                           T0[:, k, n * BANK:(n + 1) * BANK],
                                           start=(k == 0 and a is hh),
                                           stop=(k == KB - 1 and a is hl))
                        if k == KB - 1:
                            mm.then_inc(s_acc, 1)

            def mix(g, n, parity, layer):
                m = NH * g + n
                need(pe, s_res, m)
                if isinstance(g, int) and g == 0:
                    pe.wait_ge(s_ylt0, n + 1)
                elif layer == 0:
                    pe.wait_ge(s_yl0, m - NH + 1)
                else:
                    pe.wait_ge(s_yl1, m - NH * NT + 1)
                if n == 0:
                    pe.wait_ge(s_mixl, g + 1)
                pe.matmul(z[:, :], mix_h[:, parity, :], yh[:, n, :], start=True, stop=False)
                pe.matmul(z[:, :], mix_h[:, parity, :], yl[:, n, :], start=False, stop=False)
                pe.matmul(z[:, :], mix_l[:, parity, :], yh[:, n, :], start=False, stop=True
                          ).then_inc(s_z, 1)

            def turn_w(d, parity, o):
                pe.wait_ge(s_wn, d + 1)
                need(pe, s_Wl, d)
                for j in range(HB):
                    k = parity * HB + j
                    pe.matmul(wT[:, j, :], side_p[:, parity, j * P:(j + 1) * P], ident[:, :],
                              is_transpose=True, start=True, stop=False)
                    mm = pe.matmul(wT[:, j, :], loraA[:, k * P:(k + 1) * P],
                                   loraB[:, bass.ds(o * P, P)], start=False, stop=True)
                mm.then_inc(s_wT, 1)

            pe.wait_ge(s_ident, 1)
            turn_x(0, 0)
            pe.wait_ge(s_b4, 5)
            for o in range(KB):
                mm = pe.transpose(line[o // HB][:, o % HB * P:(o % HB + 1) * P], b_wide[:, o, :],
                                  ident[:, :])
                if o % HB == HB - 1:
                    mm.then_inc(s_bT, 1)

            def one(g, parity, layer):
                if isinstance(g, int) and g == 0:
                    main_first()
                    return
                if exists(g + 1):
                    loop["gi"] = half_index(g, 1, parity, loop)
                    turn_x(g + 1, 1 - parity)
                main(g, 0, parity, layer)
                if isinstance(g, int) and g == 1:
                    pe.wait_ge(s_sum, KB)
                    pe.wait_ge(s_fill, 3)
                    pe.wait_ge(s_hl, NH * 3)
                    for n in range(NH):
                        pe.matmul(col_sum[n], ones, col_scale[:, n * BANK:(n + 1) * BANK],
                                  start=True, stop=True).then_inc(s_colsum, 1)
                if exists(g - 1):
                    mix(g - 1, 0, 1 - parity, layer_of(g - 1, layer))
                first_piece = isinstance(g, int) and g == 1
                if not first_piece and has_piece(g - 1, layer):
                    turn_w(g - 1, 1 - parity, half_index(g, -1, parity, loop))
                main(g, 1, parity, layer)
                if first_piece:
                    pe.wait_ge(s_colscale, NH)
                    pe.wait_ge(s_loraB, NH)
                    pe.wait_ge(s_al, 1)
                    turn_w(0, 0, 0)
                if exists(g - 1):
                    mix(g - 1, 1, 1 - parity, layer_of(g - 1, layer))

            steps(pe, one, loop)
            mix(LAST, 0, LAST % 2, 1)
            mix(LAST, 1, LAST % 2, 1)


def kernel(**inputs):
    import numpy as _np
    import concourse.bacc as _bacc
    from concourse import mybir as _mybir
    from concourse.bass_utils import run_bass_kernel_spmd as _run

    names = ["x", "itok_B_0_15", "L0_cond_weights", "L0_ffn_w", "L0_ffn_b", "L1_cond_weights",
             "L1_ffn_q_weight", "L1_ffn_q_scale", "L1_ffn_bias", "L1_ffn_lora_A", "L1_ffn_lora_B"]
    nc = _bacc.Bacc("TRN2", target_bir_lowering=False, num_devices=1, dynamic_dma_scratch_size=1024)
    arrays, args = {}, []
    for name in names:
        a = _np.ascontiguousarray(inputs[name])
        arrays[f"in_{name}"] = a
        args.append(nc.dram_tensor(f"in_{name}", a.shape, _mybir.dt.from_np(a.dtype),
                                   kind="ExternalInput").ap())
    shape = arrays["in_x"].shape
    args.append(nc.dram_tensor("out_0", shape, _mybir.dt.float32, kind="ExternalOutput").ap())
    build(nc, *args)
    r = _run(nc, [arrays], core_ids=[0])
    return r.results[0]["out_0"]
```

```python
from contextlib import ExitStack

import numpy as np

import concourse.bass as bass
from concourse import mybir

F32 = mybir.dt.float32
F32R = mybir.dt.float32r
I32 = mybir.dt.int32
I8 = mybir.dt.int8
ALU = mybir.AluOpType
ACT = mybir.ActivationFunctionType

P = 128
BANK = 512
THRESHOLD = 0.05
LORA_SCALING = 32.0 / 8.0
NF4_LEVELS = [-1.0, -0.6961928009986877, -0.5250730514526367, -0.39491748809814453,
              -0.28444138169288635, -0.18477343022823334, -0.09105003625154495, 0.0,
              0.07958029955625534, 0.16093020141124725, 0.24611230194568634, 0.33791524171829224,
              0.44070982933044434, 0.5626170039176941, 0.7229568362236023, 1.0]
NF4_ZERO = 7


def line_through(a, level_a, b, level_b):
    f = np.float32
    want = (f(level_a), f(level_b))

    def near(v):
        up = down = f(v)
        yield up
        for _ in range(200):
            up, down = np.nextafter(up, f(9)), np.nextafter(down, f(-9))
            yield up
            yield down

    for slope in near((float(level_b) - float(level_a)) / (b - a)):
        for offset in near(float(level_a) - a * float(slope)):
            if all(f(q * float(slope) + float(offset)) == w for q, w in zip((a, b), want)):
                return float(slope), float(offset)
    raise ValueError("no such line")


def nf4_lines():
    lv = [np.float32(x) for x in NF4_LEVELS]
    z = NF4_ZERO
    above = [line_through(k, lv[z + k], k + 1, lv[z + k + 1]) for k in (1, 3, 5, 7)]
    below = [line_through(-k, -lv[z - k], -k - 1, -lv[z - k - 1]) for k in (1, 3, 5)]
    below.append((-0.5, 1.0 - 0.5 * z))
    for q in range(16):
        d = q - z
        up = max(0.0, *(np.float32(d * s + o) for s, o in above))
        down = max(0.0, *(np.float32(d * s + o) for s, o in below))
        assert np.float32(up) - np.float32(down) == lv[q]
    return above, below


def build(nc, x, itok, mix0, w0, b0, mix1, q_weight, q_scale, b1, lora_a, lora_b, out):
    B, C, T = x.shape
    NCOND = mix0.shape[0]
    G = q_scale.shape[0] // T
    R = lora_a.shape[0]
    NT = B * C // P
    KB = T // P
    NH = T // BANK
    HB = KB // NH
    ND = KB * NH
    GH = G // NH
    NL = 4
    NC = NL - 1
    LR = 2
    LEAD = 2
    assert C * 2 == P and NH == 2 and ND == NT and G == 16 and R == 8
    above, below = nf4_lines()

    x_v = x.rearrange("(t s) c f -> t (s c) f", s=2)
    out_v = out.rearrange("(t s) c f -> t (s c) f", s=2)
    w0_v = w0.rearrange("(k p) o -> k p o", p=P)
    q_v = q_weight.rearrange("(o p) (h i) -> o h p i", p=P, h=NH)
    scale_v = q_scale.rearrange("(o p g) -> p o g", p=P, g=G)
    lora_b_v = lora_b.rearrange("(o p) r -> p o r", p=P)

    with ExitStack() as ctx:
        def sb(name, shape, dt):
            return ctx.enter_context(nc.sbuf_tensor(name, shape, dt))

        def ps(name, shape):
            return ctx.enter_context(nc.psum_tensor(name, shape, F32))

        def sem(name):
            return ctx.enter_context(nc.semaphore(name))

        X = sb("X", [P, NT, T], F32)
        xin = sb("xin", [P, 2, T], F32)
        T0 = sb("T0", [P, KB, T], F32R)
        Wh = sb("Wh", [P, KB, T], F32R)
        Wl = sb("Wl", [P, KB, T], F32R)
        hh = sb("hh", [P, 2, KB, P], F32R)
        hl = sb("hl", [P, 2, KB, P], F32R)
        ys = sb("ys", [P, BANK], F32)
        yh = sb("yh", [P, NH, BANK], F32R)
        yl = sb("yl", [P, NH, BANK], F32R)
        col_scale = sb("col_scale", [P, T], F32)
        bias = sb("bias", [P, T], F32)
        mix_raw = sb("mix_raw", [P, P], F32)
        mix_h = sb("mix_h", [P, 2, P], F32R)
        mix_l = sb("mix_l", [P, 2, P], F32R)
        loraA = sb("loraA", [P, T], F32R)
        loraB = sb("loraB", [P, T], F32R)
        scales = sb("scales", [P, KB, G], F32)
        ident = sb("ident", [P, P], F32)
        q_raw = sb("q_raw", [P, BANK], I32)
        q_mid = sb("q_mid", [P, 2, BANK], I8)
        side_p = sb("side_p", [P, 2, BANK], F32)
        side_n = sb("side_n", [P, BANK], F32)
        tok = sb("tok", [1, B], I32)

        def w_raw(k):
            return X[:, NT - KB + k, :]
        ones = X[:, 7, 0:P]
        a_raw = X[:, 6, :]
        b_wide = X[:, 5, :].rearrange("p (o r) -> p o r", o=KB)
        b_raw = X[:, 4, 0:KB * R].rearrange("p (o r) -> p o r", o=KB)

        xT = [ps(f"xT{h}", [P, HB, P]) for h in range(NH)]
        acc = [ps(f"acc{n}", [P, BANK]) for n in range(NH)]
        z = ps("z", [P, BANK])
        wT = ps("wT", [P, HB, P])
        line = [ps(f"line{j}", [P, BANK]) for j in range(LR)]
        wT_flat = wT[:, :, :].rearrange("p b c -> p (b c)")
        xT_flat = xT[1][:, :, :].rearrange("p b c -> p (b c)")
        z_last = [z[:, :], xT[0][:, :, :].rearrange("p b c -> p (b c)"), xT_flat]
        NP = 2
        PART = BANK // NP
        acc_part = [acc[1][:, 0:PART], line[0][:, 0:PART]]
        z_part = [z[:, 0:PART], wT_flat[:, 0:PART]]
        col_sum = [wT_flat, xT_flat]

        s_tok = sem("s_tok")
        s_xin = [sem(f"s_xin{k}") for k in range(2)]
        s_win = [sem(f"s_win{k}") for k in range(KB)]
        s_mixin = sem("s_mixin")
        s_b0 = sem("s_b0")
        s_b1 = sem("s_b1")
        s_scales = sem("s_scales")
        s_ain = sem("s_ain")
        s_bin = sem("s_bin")
        s_qin = sem("s_qin")
        s_out = sem("s_out")
        s_zero = sem("s_zero")
        s_ident = sem("s_ident")
        s_fill = sem("s_fill")
        s_settled = sem("s_settled")
        s_xb = sem("s_xb")
        s_xT = sem("s_xT")
        s_hh = sem("s_hh")
        s_hl = sem("s_hl")
        s_acc = sem("s_acc")
        s_ys = sem("s_ys")
        s_yh = sem("s_yh")
        s_ylt0 = sem("s_ylt0")
        s_yl0 = sem("s_yl0")
        s_yl1 = sem("s_yl1")
        s_mixh = sem("s_mixh")
        s_mixl = sem("s_mixl")
        s_z = sem("s_z")
        s_zs = sem("s_zs")
        s_res = sem("s_res")
        s_neg = sem("s_neg")
        s_T0 = sem("s_T0")
        s_sign = sem("s_sign")
        s_abs = sem("s_abs")
        s_abs2 = sem("s_abs2")
        s_sum = sem("s_sum")
        s_colsum = sem("s_colsum")
        s_colscale = sem("s_colscale")
        s_ah = sem("s_ah")
        s_al = sem("s_al")
        s_b4 = sem("s_b4")
        s_bT = sem("s_bT")
        s_loraB = sem("s_loraB")
        s_qmid = sem("s_qmid")
        s_line = sem("s_line")
        s_max = sem("s_max")
        s_lev = sem("s_lev")
        s_wn = sem("s_wn")
        s_wT = sem("s_wT")
        s_Wh = sem("s_Wh")
        s_Wl = sem("s_Wl")

        LAST = 2 * NT - 1
        abs_order = [k ^ 1 for k in range(KB)]

        def need(eng, s, v):
            if not isinstance(v, int) or v > 0:
                eng.wait_ge(s, v)

        def tile_of(g, layer):
            return X[:, bass.ds(g - layer * NT, 1), :].rearrange("p a f -> p (a f)")

        def half_of(g, layer, n):
            return tile_of(g, layer)[:, n * BANK:(n + 1) * BANK]

        def exists(g):
            return not isinstance(g, int) or 0 <= g <= LAST

        def layer_of(g, layer):
            return g // NT if isinstance(g, int) else layer

        def has_piece(d, layer):
            return 0 <= d < ND if isinstance(d, int) else layer == 0

        def steps(eng, one, loop, start=None, last=None):
            for layer in range(2):
                first = layer * NT
                if start and layer == 0:
                    start()
                else:
                    one(first, 0, layer)
                    one(first + 1, 1, layer)
                with eng.Fori(first // 2 + 1, (first + NT) // 2 - 1) as i:
                    loop["i"] = i
                    for parity in range(2):
                        one(2 * i + parity, parity, layer)
                one(first + NT - 2, 0, layer)
                if last and layer == 1:
                    last()
                else:
                    one(first + NT - 1, 1, layer)

        def half_index(g, off, parity, loop):
            if isinstance(g, int):
                return (g + off) // 2
            return loop["i"] + (parity + off) // 2

        block = ctx.enter_context(nc.Block())

        @block.sync
        def _(sp):
            loop = {}

            def load_x(g, parity, layer):
                need(sp, s_xT, NH * (g - 1))
                need(sp, s_xb, g - 1)
                if layer == 0:
                    src = x_v[bass.ds(g, 1)].rearrange("a p f -> p (a f)")
                else:
                    sp.wait_ge(s_res, NH * (g - NT + 1))
                    src = tile_of(g, layer)
                sp.dma_start(xin[:, parity, :], src).then_inc(s_xin[parity], 16)

            def load_mix(g, layer):
                need(sp, s_mixl, g)
                table = mix1 if layer else mix0
                for s in range(2):
                    c = sp.value_load(tok[0:1, bass.ds(2 * (g - layer * NT) + s, 1)],
                                      min_val=0, max_val=NCOND - 1)
                    sp.dma_start(mix_raw[s * C:(s + 1) * C, s * C:(s + 1) * C],
                                 table[bass.ds(c, 1)].rearrange("a c d -> c (a d)")
                                 ).then_inc(s_mixin, 16)

            def load_q(d, o, parity):
                need(sp, s_qmid, d)
                sp.dma_start(q_raw[:, :], q_v[bass.ds(o, 1), parity].rearrange("a p i -> p (a i)")
                             ).then_inc(s_qin, 16)

            def store(g):
                sp.wait_ge(s_res, NH * (g + 1))
                sp.dma_start(out_v[bass.ds(g - NT, 1)].rearrange("a p f -> p (a f)"),
                             tile_of(g, 1)).then_inc(s_out, 16)

            load_x(0, 0, 0)
            for k in range(KB):
                sp.dma_start(w_raw(k), w0_v[k]).then_inc(s_win[k], 16)
                if k == 3:
                    sp.dma_start(bias[:, :], b0.rearrange("(a f) -> a f", a=1).to_broadcast([P, T])
                                 ).then_inc(s_b0, 16)
                    sp.dma_start(tok[:, :], itok.rearrange("(a b) -> a b", a=1)).then_inc(s_tok, 16)
            load_x(1, 1, 0)
            load_q(0, 0, 0)
            sp.wait_ge(s_tok, 16)
            sp.wait_ge(s_fill, 4)
            load_mix(0, 0)
            for r in range(4):
                sp.dma_start(a_raw[32 * r:32 * r + R, :], lora_a).then_inc(s_ain, 16)
            sp.dma_start(scales[:, :, :], scale_v).then_inc(s_scales, 16)

            def one(g, parity, layer):
                if exists(g + 2):
                    load_x(g + 2, parity, layer_of(g + 2, layer))
                if has_piece(g + 1, layer):
                    load_q(g + 1, half_index(g, 1, parity, loop), 1 - parity)
                if layer == 0 and isinstance(g, int) and g == NT - 2:
                    sp.wait_ge(s_xb, NT)
                    sp.dma_start(bias[:, :], b1.rearrange("(a f) -> a f", a=1).to_broadcast([P, T])
                                 ).then_inc(s_b1, 16)
                if exists(g + 1):
                    load_mix(g + 1, layer_of(g + 1, layer))
                if layer == 1 and not (isinstance(g, int) and g - 2 < NT):
                    store(g - 2)

            steps(sp, one, loop)
            store(LAST - 1)
            done = 0
            for j, width in enumerate([BANK] + [PART] * NP):
                sp.wait_ge(s_res, NH * LAST + 1 + j)
                sp.dma_start(out_v[NT - 1][:, done:done + width],
                             tile_of(LAST, 1)[:, done:done + width]).then_inc(s_out, 16)
                done += width
            sp.wait_ge(s_out, 16 * (NT + NP))

        @block.gpsimd
        def _(pool):
            loop = {}

            def settle():
                pool.sem_inc(s_settled, 1)

            def add_bias(g, parity, layer):
                pool.wait_ge(s_xin[parity], 16 * ((g // 2 if isinstance(g, int) else loop["gi"])
                                                  + 1))
                if isinstance(g, int) and g == 0:
                    pool.wait_ge(s_b0, 16)
                if isinstance(g, int) and g == NT:
                    pool.wait_ge(s_b1, 16)
                settle()
                pool.tensor_tensor(tile_of(g, layer), xin[:, parity, :], bias[:, :], ALU.add
                                   ).then_inc(s_xb, 1)

            def low_y(g, n):
                pool.wait_ge(s_yh, NH * g + n + 1)
                settle()
                pool.tensor_tensor(yl[:, n, :], ys[:, :], yh[:, n, :].bitcast(F32), ALU.subtract
                                   ).then_inc(s_yl0, 1)

            def weight(d, parity, o):
                lev = side_p[:, parity, :]
                pool.wait_ge(s_max, 2 * NC * (d + 1))
                settle()
                pool.tensor_tensor(lev, lev, side_n[:, :], ALU.subtract).then_inc(s_lev, 1)
                pool.wait_ge(s_lev, d + 1)
                settle()
                sc = scales[:, bass.ds(o, 1), parity * GH:(parity + 1) * GH].rearrange(
                    "p a g -> p (a g)").unsqueeze(2).to_broadcast([P, GH, BANK // GH])
                lev3 = lev.rearrange("p (g i) -> p g i", g=GH)
                pool.tensor_tensor(lev3, lev3, sc, ALU.mult).then_inc(s_wn, 1)

            pool.memset(ident[:, :], 0.0).then_inc(s_zero, 1)
            pool.wait_ge(s_zero, 1)
            pool.affine_select(out=ident[:, :], in_=ident[:, :], compare_op=ALU.not_equal, fill=1.0,
                               base=0, pattern=[[-1, P]], channel_multiplier=1).then_inc(s_ident, 1)
            for j in range(1, KB - 1):
                pool.wait_ge(s_abs, j + 1)
                if j == KB - 2:
                    pool.wait_ge(s_abs2, 1)
                if j == 2:
                    add_bias(0, 0, 0)
                if j == 1:
                    pool.tensor_tensor(col_scale[:, :], w_raw(abs_order[0]), w_raw(abs_order[1]),
                                       ALU.add).then_inc(s_sum, 1)
                else:
                    pool.wait_ge(s_sum, j - 1)
                    pool.tensor_tensor(col_scale[:, :], col_scale[:, :], w_raw(abs_order[j]),
                                       ALU.add).then_inc(s_sum, 1)
            pool.wait_ge(s_scales, 16)

            def one(g, parity, layer):
                if exists(g + 1):
                    loop["gi"] = half_index(g, 1, parity, loop)
                    add_bias(g + 1, 1 - parity, layer_of(g + 1, layer))
                if isinstance(g, int) and g == 0:
                    pool.wait_ge(s_xb, 2)
                    pool.wait_ge(s_ah, 1)
                    pool.tensor_tensor(loraA[64:P, :], a_raw[64:P, :], loraA[64:P, :].bitcast(F32),
                                       ALU.subtract).then_inc(s_al, 1)
                    pool.wait_ge(s_al, 1)
                if layer == 0:
                    if not (isinstance(g, int) and g == 0):
                        low_y(g, 0)
                    weight(g, parity, half_index(g, 0, parity, loop))
                    if not (isinstance(g, int) and g == 0):
                        low_y(g, 1)

            steps(pool, one, loop)

        @block.scalar
        def _(act):
            loop = {}

            def high_x(g, parity):
                for h in range(NH):
                    act.wait_ge(s_xT, NH * g + h + 1)
                    if h == 0:
                        need(act, s_acc, NH * (g - 1))
                    act.activation(hh[:, parity, h * HB:(h + 1) * HB, :], xT[h][:, :, :], ACT.Copy
                                   ).then_inc(s_hh, 1)

            def high_mix(g, parity):
                act.wait_ge(s_mixin, 32 * (g + 1))
                need(act, s_z, NH * (g - 1))
                act.activation(mix_h[:, parity, :], mix_raw[:, :], ACT.Copy).then_inc(s_mixh, 1)

            def high_y(g, n, layer):
                m = NH * g + n
                need(act, s_z, m - 1)
                if layer == 0 and not (isinstance(g, int) and g == 0):
                    act.wait_ge(s_ys, m - NH + 1)
                    src = ys[:, :]
                else:
                    act.wait_ge(s_acc, m + 1)
                    src = acc[n][:, :]
                act.activation(yh[:, n, :], src, ACT.Copy).then_inc(s_yh, 1)

            def lines(d, parity, start, stop):
                if start == 0:
                    act.wait_ge(s_qin, 16 * (d + 1))
                    need(act, s_line, 2 * NL * (d - 1))
                    act.activation(q_mid[:, parity, :], q_raw[:, :], ACT.Copy,
                                   bias=-float(NF4_ZERO)).then_inc(s_qmid, 1)
                    act.wait_ge(s_qmid, d + 1)
                for number in range(start, stop):
                    side, j = divmod(number, NL)
                    slope, offset = (above, below)[side][j]
                    if j == 0 and side == 0:
                        need(act, s_wT, d - 1)
                        dst = side_p[:, parity, :]
                    elif j == 0:
                        need(act, s_lev, d)
                        dst = side_n[:, :]
                    else:
                        c = NC * side + j - 1
                        need(act, s_max, 2 * NC * d + c - LR + 1)
                        if isinstance(d, int) and d == 0:
                            act.wait_ge(s_loraB, NH)
                        dst = line[c % LR][:, :]
                    act.activation(dst, q_mid[:, parity, :], ACT.Copy, scale=slope, bias=offset
                                   ).then_inc(s_line, 1)

            def high_w(d, parity, o):
                act.wait_ge(s_wT, d + 1)
                act.activation(Wh[:, parity * HB:(parity + 1) * HB, bass.ds(o * P, P)], wT[:, :, :],
                               ACT.Copy).then_inc(s_Wh, 1)

            act.dma_start(b_raw, lora_b_v).then_inc(s_bin, 16)
            high_x(0, 0)
            for k in abs_order:
                if k % 2:
                    act.wait_ge(s_win[k], 16)
                    act.activation(T0[:, k, :], w_raw(k), ACT.Sign).then_inc(s_sign, 1)
                    act.wait_ge(s_sign, k // 2 + 1)
                else:
                    act.wait_ge(s_T0, k + 1)
                act.activation(w_raw(k), w_raw(k), ACT.Abs).then_inc(s_abs, 1)
                if k == KB - 1:
                    high_x(1, 1)

            def start():
                for n in range(NH):
                    high_y(0, n, 0)
                high_x(2, 0)
                high_mix(0, 0)
                for h in range(NH):
                    act.wait_ge(s_bT, h + 1)
                    act.activation(loraB[:, h * BANK:(h + 1) * BANK], line[h][:, :], ACT.Copy
                                   ).then_inc(s_loraB, 1)
                lines(0, 0, 0, 3)
                act.wait_ge(s_ain, 64)
                act.activation(loraA[:, :], a_raw, ACT.Copy).then_inc(s_ah, 1)
                lines(0, 0, 3, 6)
                for n in range(NH):
                    act.wait_ge(s_colsum, n + 1)
                    act.activation(col_scale[:, n * BANK:(n + 1) * BANK], col_sum[n], ACT.Copy,
                                   scale=1.0 / T).then_inc(s_colscale, 1)
                lines(0, 0, 6, 8)
                high_mix(1, 1)
                lines(1, 1, 0, 1)
                high_y(1, 0, 0)
                lines(1, 1, 1, 6)
                high_w(0, 0, 0)
                lines(1, 1, 6, 8)
                lines(2, 0, 0, LEAD)
                high_y(1, 1, 0)

            def one(g, parity, layer):
                if exists(g + 1):
                    high_x(g + 1, 1 - parity)
                high_mix(g, parity)
                if layer == 0:
                    lines(g, parity, LEAD, 4)
                high_y(g, 0, layer)
                if layer == 0:
                    lines(g, parity, 4, 6)
                if has_piece(g - 1, layer):
                    high_w(g - 1, 1 - parity, half_index(g, -1, parity, loop))
                if layer == 0:
                    lines(g, parity, 6, 8)
                if has_piece(g + 1, layer):
                    lines(g + 1, 1 - parity, 0, LEAD)
                high_y(g, 1, layer)

            def last():
                high_mix(LAST, LAST % 2)
                high_y(LAST, 0, 1)
                for q in range(NP):
                    act.wait_ge(s_acc, NH * LAST + 2 + q)
                    act.wait_ge(s_z, NH * LAST)
                    act.activation(yh[:, 1, q * PART:(q + 1) * PART], acc_part[q], ACT.Copy
                                   ).then_inc(s_yh, 1)

            steps(act, one, loop, start, last)

        @block.vector
        def _(dve):
            loop = {}

            def low_mix(g, parity):
                dve.wait_ge(s_mixh, g + 1)
                dve.tensor_tensor(mix_l[:, parity, :], mix_raw[:, :],
                                  mix_h[:, parity, :].bitcast(F32), ALU.subtract
                                  ).then_inc(s_mixl, 1)

            def low_x(g, parity):
                for h in range(NH):
                    dve.wait_ge(s_hh, NH * g + h + 1)
                    blocks = slice(h * HB, (h + 1) * HB)
                    dve.tensor_tensor(hl[:, parity, blocks, :], xT[h][:, :, :],
                                      hh[:, parity, blocks, :].bitcast(F32), ALU.subtract
                                      ).then_inc(s_hl, 1)

            def leave_y(g, n, layer):
                m = NH * g + n
                if isinstance(g, int) and g == 0:
                    dve.wait_ge(s_yh, n + 1)
                    dve.tensor_tensor(yl[:, n, :], acc[n][:, :], yh[:, n, :].bitcast(F32),
                                      ALU.subtract).then_inc(s_ylt0, 1)
                elif layer == 0:
                    dve.wait_ge(s_acc, m + 1)
                    need(dve, s_yl0, m - NH)
                    if isinstance(g, int) and g == 1:
                        dve.wait_ge(s_colscale, n + 1)
                    dve.tensor_tensor(ys[:, :], acc[n][:, :],
                                      col_scale[:, n * BANK:(n + 1) * BANK], ALU.mult
                                      ).then_inc(s_ys, 1)
                else:
                    dve.wait_ge(s_yh, m + 1)
                    dve.tensor_tensor(yl[:, n, :], acc[n][:, :], yh[:, n, :].bitcast(F32),
                                      ALU.subtract).then_inc(s_yl1, 1)

            def result(g, n, layer, bank=z[:, :]):
                dve.wait_ge(s_z, NH * g + n + 1)
                dve.wait_ge(s_xb, g + 1)
                t = half_of(g, layer, n)
                dve.tensor_tensor(t, t, bank, ALU.add).then_inc(s_res, 1)

            def scale_z(n):
                dve.wait_ge(s_z, n + 1)
                dve.wait_ge(s_colscale, n + 1)
                dve.tensor_tensor(z[:, :], z[:, :], col_scale[:, n * BANK:(n + 1) * BANK],
                                  ALU.mult).then_inc(s_zs, 1)
                dve.wait_ge(s_zs, n + 1)

            def maxima(d, parity, start, stop):
                for c in range(start, stop):
                    side, j = divmod(c, NC)
                    dst = side_n[:, :] if side else side_p[:, parity, :]
                    dve.wait_ge(s_line, 2 * NL * d + NL * side + j + 2)
                    if j == 0:
                        ins = dve.scalar_tensor_tensor(dst, dst, 0.0, line[c % LR][:, :],
                                                       ALU.max, ALU.max)
                    else:
                        dve.wait_ge(s_max, 2 * NC * d + c)
                        ins = dve.tensor_tensor(dst, dst, line[c % LR][:, :], ALU.max)
                    ins.then_inc(s_max, 1)

            def low_w(d, parity, o):
                dve.wait_ge(s_Wh, d + 1)
                part = (slice(None), slice(parity * HB, (parity + 1) * HB), bass.ds(o * P, P))
                dve.tensor_tensor(Wl[part], wT[:, :, :], Wh[part].bitcast(F32), ALU.subtract
                                  ).then_inc(s_Wl, 1)

            for where, value in ((X[:, 5, :], 0.0), (mix_raw[:, :], 0.0), (ones, 1.0),
                                 (a_raw, 0.0)):
                dve.memset(where, value).then_inc(s_fill, 1)
            dve.wait_ge(s_bin, 16)
            dve.wait_ge(s_fill, 1)
            dve.tensor_scalar(b_raw, b_raw, LORA_SCALING, None, ALU.mult).then_inc(s_b4, 1)
            dve.wait_ge(s_b4, 1)
            for c in (0, 64):
                dve.tensor_copy(b_wide[:, :, c:c + R].bitcast(F32R), b_raw).then_inc(s_b4, 1)
            dve.wait_ge(s_b4, 3)
            for c in (32, 96):
                dve.tensor_tensor(b_wide[:, :, c:c + R], b_raw, b_wide[:, :, 0:R],
                                  ALU.subtract).then_inc(s_b4, 1)
            for k in range(KB):
                if k % 2:
                    dve.wait_ge(s_abs, k)
                    dve.scalar_tensor_tensor(T0[:, k, :], w_raw(k), THRESHOLD,
                                             T0[:, k, :].bitcast(F32), ALU.is_ge, ALU.mult
                                             ).then_inc(s_T0, 1)
                else:
                    dve.wait_ge(s_win[k], 16)
                    dve.tensor_scalar(T0[:, k, :], w_raw(k), -THRESHOLD, None, ALU.is_le
                                      ).then_inc(s_neg, 1)
                    dve.wait_ge(s_neg, k // 2 + 1)
                    dve.scalar_tensor_tensor(T0[:, k, :], w_raw(k), THRESHOLD,
                                             T0[:, k, :].bitcast(F32), ALU.is_ge, ALU.subtract
                                             ).then_inc(s_T0, 1)
                if k == 0:
                    low_x(0, 0)
            low_x(1, 1)

            def start():
                for n in range(NH):
                    leave_y(0, n, 0)
                dve.wait_ge(s_abs, KB)
                dve.tensor_tensor(w_raw(abs_order[-2]), w_raw(abs_order[-2]),
                                  w_raw(abs_order[-1]), ALU.add).then_inc(s_abs2, 1)
                low_x(2, 0)
                low_mix(0, 0)
                maxima(0, 0, 0, 4)
                leave_y(1, 0, 0)
                maxima(0, 0, 4, 6)
                scale_z(0)
                result(0, 0, 0)
                low_mix(1, 1)
                maxima(1, 1, 0, 4)
                low_w(0, 0, 0)
                maxima(1, 1, 4, 6)
                leave_y(1, 1, 0)
                scale_z(1)
                result(0, 1, 0)

            def one(g, parity, layer):
                if exists(g + 1):
                    low_x(g + 1, 1 - parity)
                low_mix(g, parity)
                if layer == 0:
                    maxima(g, parity, 0, 1)
                leave_y(g, 0, layer)
                if layer == 0:
                    maxima(g, parity, 1, 2)
                if exists(g - 1):
                    result(g - 1, 0, layer_of(g - 1, layer))
                if layer == 0:
                    maxima(g, parity, 2, 4)
                if has_piece(g - 1, layer):
                    low_w(g - 1, 1 - parity, half_index(g, -1, parity, loop))
                if layer == 0:
                    maxima(g, parity, 4, 6)
                leave_y(g, 1, layer)
                if exists(g - 1):
                    result(g - 1, 1, layer_of(g - 1, layer))

            def low_part(q):
                dve.wait_ge(s_yh, NH * LAST + 2 + q)
                cols = slice(q * PART, (q + 1) * PART)
                dve.tensor_tensor(yl[:, 1, cols], acc_part[q], yh[:, 1, cols].bitcast(F32),
                                  ALU.subtract).then_inc(s_yl1, 1)

            def result_part(q):
                dve.wait_ge(s_z, NH * LAST + 2 + q)
                t = half_of(LAST, 1, 1)[:, q * PART:(q + 1) * PART]
                dve.tensor_tensor(t, t, z_part[q], ALU.add).then_inc(s_res, 1)

            def last():
                low_mix(LAST, LAST % 2)
                leave_y(LAST, 0, 1)
                result(LAST - 1, 0, 1, z_last[0])
                result(LAST - 1, 1, 1, z_last[1])
                low_part(0)
                result(LAST, 0, 1, z_last[2])
                low_part(1)
                result_part(0)
                result_part(1)

            steps(dve, one, loop, start, last)

        @block.tensor
        def _(pe):
            loop = {}

            def turn_x(g, parity):
                pe.wait_ge(s_xin[parity], 16 * ((g // 2 if isinstance(g, int) else loop["gi"]) + 1))
                need(pe, s_hl, NH * g)
                for k in range(KB):
                    mm = pe.transpose(xT[k // HB][:, k % HB, :], xin[:, parity, k * P:(k + 1) * P],
                                      ident[:, :])
                    if k % HB == HB - 1:
                        mm.then_inc(s_xT, 1)

            def main(g, n, parity, layer, bank=None, cols=None):
                bank = acc[n][:, :] if bank is None else bank
                cols = slice(n * BANK, (n + 1) * BANK) if cols is None else cols
                before = layer_of(g - 1, layer)
                if isinstance(g, int) and g == 1:
                    pe.wait_ge(s_ylt0, n + 1)
                elif before == 0:
                    pe.wait_ge(s_ys, NH * (g - 2) + n + 1)
                else:
                    pe.wait_ge(s_yl1, NH * (g - 1 - NT) + n + 1)
                if n == 0:
                    pe.wait_ge(s_hl, NH * (g + 1))
                if layer == 0:
                    terms = [(hh, T0), (hl, T0)]
                else:
                    terms = [(hh, Wh), (hl, Wh), (hh, Wl)]
                for k in range(KB):
                    if isinstance(g, int) and g == NT and k % HB == 0:
                        pe.wait_ge(s_Wl, ND // NH * (n + 1) - 1 + k // HB)
                    for j, (a, b) in enumerate(terms):
                        mm = pe.matmul(bank, a[:, parity, k, :], b[:, k, cols],
                                       start=(k == 0 and j == 0),
                                       stop=(k == KB - 1 and j == len(terms) - 1))
                mm.then_inc(s_acc, 1)

            def main_first():
                pe.wait_ge(s_hl, NH)
                for k in range(KB):
                    if k == KB - 2:
                        turn_x(1, 1)
                    pe.wait_ge(s_T0, k + 1)
                    for n in range(NH):
                        for a in (hh, hl):
                            mm = pe.matmul(acc[n][:, :], a[:, 0, k, :],
                                           T0[:, k, n * BANK:(n + 1) * BANK],
                                           start=(k == 0 and a is hh),
                                           stop=(k == KB - 1 and a is hl))
                        if k == KB - 1:
                            mm.then_inc(s_acc, 1)

            def mix(g, n, parity, layer, bank=None):
                m = NH * g + n
                if bank is None:
                    need(pe, s_res, m)
                    bank = z[:, :]
                if isinstance(g, int) and g == 0:
                    pe.wait_ge(s_ylt0, n + 1)
                elif layer == 0:
                    pe.wait_ge(s_yl0, m - NH + 1)
                else:
                    pe.wait_ge(s_yl1, m - NH * NT + 1)
                if n == 0:
                    pe.wait_ge(s_mixl, g + 1)
                mix_terms(bank, parity, n, slice(0, BANK))

            def mix_terms(bank, parity, n, cols):
                terms = [(mix_h, yh), (mix_h, yl), (mix_l, yh)]
                for j, (a, b) in enumerate(terms):
                    mm = pe.matmul(bank, a[:, parity, :], b[:, n, cols], start=(j == 0),
                                   stop=(j == len(terms) - 1))
                mm.then_inc(s_z, 1)

            def turn_w(d, parity, o):
                pe.wait_ge(s_wn, d + 1)
                need(pe, s_Wl, d)
                for j in range(HB):
                    k = parity * HB + j
                    pe.matmul(wT[:, j, :], side_p[:, parity, j * P:(j + 1) * P], ident[:, :],
                              is_transpose=True, start=True, stop=False)
                    mm = pe.matmul(wT[:, j, :], loraA[:, k * P:(k + 1) * P],
                                   loraB[:, bass.ds(o * P, P)], start=False, stop=True)
                mm.then_inc(s_wT, 1)

            pe.wait_ge(s_ident, 1)
            turn_x(0, 0)
            pe.wait_ge(s_b4, 5)
            for o in range(KB):
                mm = pe.transpose(line[o // HB][:, o % HB * P:(o % HB + 1) * P], b_wide[:, o, :],
                                  ident[:, :])
                if o % HB == HB - 1:
                    mm.then_inc(s_bT, 1)

            def start():
                main_first()
                turn_x(2, 0)
                main(1, 0, 1, 0)
                pe.wait_ge(s_sum, KB - 2)
                pe.wait_ge(s_fill, 3)
                pe.wait_ge(s_hl, NH * 3)
                for n in range(NH):
                    pe.matmul(col_sum[n], ones, col_scale[:, n * BANK:(n + 1) * BANK],
                              start=True, stop=True).then_inc(s_colsum, 1)
                mix(0, 0, 0, 0)
                main(1, 1, 1, 0)
                mix(0, 1, 0, 0)
                pe.wait_ge(s_colscale, NH)
                pe.wait_ge(s_loraB, NH)
                pe.wait_ge(s_al, 1)
                turn_w(0, 0, 0)

            def one(g, parity, layer):
                if exists(g + 1):
                    loop["gi"] = half_index(g, 1, parity, loop)
                    turn_x(g + 1, 1 - parity)
                main(g, 0, parity, layer)
                if exists(g - 1):
                    mix(g - 1, 0, 1 - parity, layer_of(g - 1, layer))
                if has_piece(g - 1, layer):
                    turn_w(g - 1, 1 - parity, half_index(g, -1, parity, loop))
                main(g, 1, parity, layer)
                if exists(g - 1):
                    mix(g - 1, 1, 1 - parity, layer_of(g - 1, layer))

            def last():
                parity = LAST % 2
                main(LAST, 0, parity, 1)
                mix(LAST - 1, 0, 1 - parity, 1)
                mix(LAST - 1, 1, 1 - parity, 1, z_last[1])
                for q in range(NP):
                    main(LAST, 1, parity, 1, acc_part[q],
                         slice(BANK + q * PART, BANK + (q + 1) * PART))
                    if q == 0:
                        mix(LAST, 0, parity, 1, z_last[2])
                pe.wait_ge(s_res, NH * (LAST - 1) + 1)
                for q in range(NP):
                    pe.wait_ge(s_yl1, NH * (LAST - NT) + 2 + q)
                    mix_terms(z_part[q], parity, 1, slice(q * PART, (q + 1) * PART))

            steps(pe, one, loop, start, last)


def kernel(**inputs):
    import numpy as _np
    import concourse.bacc as _bacc
    from concourse import mybir as _mybir
    from concourse.bass_utils import run_bass_kernel_spmd as _run

    names = ["x", "itok_B_0_15", "L0_cond_weights", "L0_ffn_w", "L0_ffn_b", "L1_cond_weights",
             "L1_ffn_q_weight", "L1_ffn_q_scale", "L1_ffn_bias", "L1_ffn_lora_A", "L1_ffn_lora_B"]
    nc = _bacc.Bacc("TRN2", target_bir_lowering=False, num_devices=1, dynamic_dma_scratch_size=1024)
    arrays, args = {}, []
    for name in names:
        a = _np.ascontiguousarray(inputs[name])
        arrays[f"in_{name}"] = a
        args.append(nc.dram_tensor(f"in_{name}", a.shape, _mybir.dt.from_np(a.dtype),
                                   kind="ExternalInput").ap())
    shape = arrays["in_x"].shape
    args.append(nc.dram_tensor("out_0", shape, _mybir.dt.float32, kind="ExternalOutput").ap())
    build(nc, *args)
    r = _run(nc, [arrays], core_ids=[0])
    return r.results[0]["out_0"]
```
